# Optimizing a Trainium2 kernel written in Bass

```python
import numpy as np
import jax
import jax.numpy as jnp

def _softmax(x, axis=-1):
    return jax.nn.softmax(x, axis=axis)

def _gelu(x):
    return jax.nn.gelu(x, approximate=True)

def _silu(x):
    return jax.nn.silu(x)

def _sigmoid(x):
    return jax.nn.sigmoid(x)

def _layernorm(x, axis=-1, eps=1e-05):
    m = jnp.mean(x, axis=axis, keepdims=True)
    v = jnp.var(x, axis=axis, keepdims=True)
    return (x - m) / jnp.sqrt(v + eps)

def _scatter_add(tgt, idx, src, axis=0):
    return tgt.at[idx].add(src)

def _segment_sum(src, seg, n):
    return jax.ops.segment_sum(src, seg, n)
kernel_name = 'mk_gnn_resnorm_d2_gnn_r8_9ca7ea'

def setup_inputs(seed: int=0):
    np.random.seed(seed)
    _w = jnp.asarray

    def _rec_inputs():
        import jax
        import jax.numpy as jnp
        _gk = jax.random.key(seed)
        x = -1.686e-05 + 1 * jax.random.normal(jax.random.fold_in(_gk, 1), (12500, 160), jnp.float32)
        src = jax.random.randint(jax.random.fold_in(_gk, 2), (200000,), 0, 12500, jnp.int32)
        dst = jax.random.randint(jax.random.fold_in(_gk, 3), (200000,), 0, 12500, jnp.int32)
        _o = jnp.argsort(dst, stable=True)
        src = src[_o]
        dst = dst[_o]
        edge_attr_4 = 0.0007022 + 0.999661 * jax.random.normal(jax.random.fold_in(_gk, 11), (200000, 4), jnp.float32)
        node_vec1 = -0.00915711 + 0.999674 * jax.random.normal(jax.random.fold_in(_gk, 13), (12500, 1), jnp.float32)
        return (x, src, dst, edge_attr_4, node_vec1)
    x, src, dst, edge_attr_4, node_vec1 = _rec_inputs()

    def _L0_gnn_setup():
        import jax, jax.numpy as jnp
        import numpy as np
        MUL0, MUL1 = (64, 32)
        INV_SQRT3 = 1.0 / np.sqrt(3.0)

        def _split(x):
            return (x[:, :MUL0], x[:, MUL0:].reshape(x.shape[0], MUL1, 3))

        def _merge(o0, o1):
            return jnp.concatenate([o0, o1.reshape(o1.shape[0], -1)], axis=-1)

        def _tp(x0, x1, y0, y1, w000, w011, w101, w110):
            fan0 = x0.shape[1] * y0.shape[1] + x1.shape[1] * y1.shape[1]
            fan1 = x0.shape[1] * y1.shape[1] + x1.shape[1] * y0.shape[1]
            out0 = (jnp.einsum('eu,ev,uvw->ew', x0, y0, w000) + INV_SQRT3 * jnp.einsum('euk,evk,uvw->ew', x1, y1, w110)) / np.sqrt(fan0)
            out1 = (jnp.einsum('eu,evk,uvw->ewk', x0, y1, w011) + jnp.einsum('euk,ev,uvw->ewk', x1, y0, w101)) / np.sqrt(fan1)
            return (out0, out1)

        def _lin(x0, x1, w0, w1):
            return (x0 @ w0 / np.sqrt(x0.shape[1]), jnp.einsum('euk,uv->evk', x1, w1) / np.sqrt(x1.shape[1]))
        key = jax.random.key(seed)
        ks = jax.random.split(key, 20)
        N, E = (6250, 62500)
        inp = {'node_features': jax.random.normal(ks[0], (N, MUL0 + 3 * MUL1), dtype=jnp.float32), 'edge_index': jax.random.randint(ks[1], (2, E), 0, N, dtype=jnp.int64), 'edge_attr_tensor': jax.random.normal(ks[2], (E, 4), dtype=jnp.float32), 'node_attr_scalar_raw': jax.random.normal(ks[3], (N, 1), dtype=jnp.float32), 'wm000': jax.random.normal(ks[4], (MUL0, 1, MUL0), dtype=jnp.float32), 'wm011': jax.random.normal(ks[5], (MUL0, 1, MUL1), dtype=jnp.float32), 'wm101': jax.random.normal(ks[6], (MUL1, 1, MUL1), dtype=jnp.float32), 'wm110': jax.random.normal(ks[7], (MUL1, 1, MUL0), dtype=jnp.float32), 'lm0': jax.random.normal(ks[8], (MUL0, MUL0), dtype=jnp.float32), 'lm1': jax.random.normal(ks[9], (MUL1, MUL1), dtype=jnp.float32), 'wu000': jax.random.normal(ks[10], (MUL0, MUL0, MUL0), dtype=jnp.float32), 'wu011': jax.random.normal(ks[11], (MUL0, MUL1, MUL1), dtype=jnp.float32), 'wu101': jax.random.normal(ks[12], (MUL1, MUL0, MUL1), dtype=jnp.float32), 'wu110': jax.random.normal(ks[13], (MUL1, MUL1, MUL0), dtype=jnp.float32), 'lu0': jax.random.normal(ks[14], (MUL0, MUL0), dtype=jnp.float32), 'lu1': jax.random.normal(ks[15], (MUL1, MUL1), dtype=jnp.float32)}
        return inp
    _L0_gnn_all = _L0_gnn_setup()
    _L0_gnn_in = {k: v for k, v in _L0_gnn_all.items() if k in ('wm000', 'wm011', 'wm101', 'wm110', 'lm0', 'lm1', 'wu000', 'wu011', 'wu101', 'wu110', 'lu0', 'lu1')}
    del _L0_gnn_all

    def _L1_gnn_setup():
        import jax, jax.numpy as jnp
        import numpy as np
        N = 2500
        E = 80000
        INV_SQRT3 = 0.5773502691896258
        INV8 = 0.125
        INV_SQRT32 = 0.17677669529663687
        INV64 = 0.015625
        INV32 = 0.03125
        INV_SQRT2048 = 0.022097086912079608
        key = jax.random.key(seed)
        ks = jax.random.split(key, 16)
        f32 = jnp.float32
        return {'node_features': jax.random.normal(ks[0], (N, 160), f32), 'edge_index': jax.random.randint(ks[1], (2, E), 0, N), 'edge_attr_tensor': jax.random.normal(ks[2], (E, 4), f32), 'node_attr_scalar_raw': jax.random.normal(ks[3], (N, 1), f32), 'Wm_ss': jax.random.normal(ks[4], (64, 64), f32), 'Wm_vv': jax.random.normal(ks[5], (32, 64), f32), 'Wm_sv': jax.random.normal(ks[6], (64, 32), f32), 'Wm_vs': jax.random.normal(ks[7], (32, 32), f32), 'Lm_s': jax.random.normal(ks[8], (64, 64), f32), 'Lm_v': jax.random.normal(ks[9], (32, 32), f32), 'Wu_ss': jax.random.normal(ks[10], (64, 64, 64), f32), 'Wu_vv': jax.random.normal(ks[11], (32, 32, 64), f32), 'Wu_sv': jax.random.normal(ks[12], (64, 32, 32), f32), 'Wu_vs': jax.random.normal(ks[13], (32, 64, 32), f32), 'Lu_s': jax.random.normal(ks[14], (64, 64), f32), 'Lu_v': jax.random.normal(ks[15], (32, 32), f32)}
    _L1_gnn_all = _L1_gnn_setup()
    _L1_gnn_in = {k: v for k, v in _L1_gnn_all.items() if k in ('Wm_ss', 'Wm_vv', 'Wm_sv', 'Wm_vs', 'Lm_s', 'Lm_v', 'Wu_ss', 'Wu_vv', 'Wu_sv', 'Wu_vs', 'Lu_s', 'Lu_v')}
    del _L1_gnn_all
    return {'x': x, 'src': src, 'dst': dst, 'edge_attr_4': edge_attr_4, 'node_vec1': node_vec1, 'L0_gnn_wm000': _L0_gnn_in['wm000'], 'L0_gnn_wm011': _L0_gnn_in['wm011'], 'L0_gnn_wm101': _L0_gnn_in['wm101'], 'L0_gnn_wm110': _L0_gnn_in['wm110'], 'L0_gnn_lm0': _L0_gnn_in['lm0'], 'L0_gnn_lm1': _L0_gnn_in['lm1'], 'L0_gnn_wu000': _L0_gnn_in['wu000'], 'L0_gnn_wu011': _L0_gnn_in['wu011'], 'L0_gnn_wu101': _L0_gnn_in['wu101'], 'L0_gnn_wu110': _L0_gnn_in['wu110'], 'L0_gnn_lu0': _L0_gnn_in['lu0'], 'L0_gnn_lu1': _L0_gnn_in['lu1'], 'L1_gnn_Wm_ss': _L1_gnn_in['Wm_ss'], 'L1_gnn_Wm_vv': _L1_gnn_in['Wm_vv'], 'L1_gnn_Wm_sv': _L1_gnn_in['Wm_sv'], 'L1_gnn_Wm_vs': _L1_gnn_in['Wm_vs'], 'L1_gnn_Lm_s': _L1_gnn_in['Lm_s'], 'L1_gnn_Lm_v': _L1_gnn_in['Lm_v'], 'L1_gnn_Wu_ss': _L1_gnn_in['Wu_ss'], 'L1_gnn_Wu_vv': _L1_gnn_in['Wu_vv'], 'L1_gnn_Wu_sv': _L1_gnn_in['Wu_sv'], 'L1_gnn_Wu_vs': _L1_gnn_in['Wu_vs'], 'L1_gnn_Lu_s': _L1_gnn_in['Lu_s'], 'L1_gnn_Lu_v': _L1_gnn_in['Lu_v']}

def reference(x, src, dst, edge_attr_4, node_vec1, L0_gnn_wm000, L0_gnn_wm011, L0_gnn_wm101, L0_gnn_wm110, L0_gnn_lm0, L0_gnn_lm1, L0_gnn_wu000, L0_gnn_wu011, L0_gnn_wu101, L0_gnn_wu110, L0_gnn_lu0, L0_gnn_lu1, L1_gnn_Wm_ss, L1_gnn_Wm_vv, L1_gnn_Wm_sv, L1_gnn_Wm_vs, L1_gnn_Lm_s, L1_gnn_Lm_v, L1_gnn_Wu_ss, L1_gnn_Wu_vv, L1_gnn_Wu_sv, L1_gnn_Wu_vs, L1_gnn_Lu_s, L1_gnn_Lu_v):
    import jax
    import jax.numpy as jnp

    def _L0_gnn_ref(node_features, edge_index, edge_attr_tensor, node_attr_scalar_raw, wm000, wm011, wm101, wm110, lm0, lm1, wu000, wu011, wu101, wu110, lu0, lu1):
        import jax, jax.numpy as jnp
        import numpy as np
        MUL0, MUL1 = (64, 32)
        INV_SQRT3 = 1.0 / np.sqrt(3.0)

        def _split(x):
            return (x[:, :MUL0], x[:, MUL0:].reshape(x.shape[0], MUL1, 3))

        def _merge(o0, o1):
            return jnp.concatenate([o0, o1.reshape(o1.shape[0], -1)], axis=-1)

        def _tp(x0, x1, y0, y1, w000, w011, w101, w110):
            fan0 = x0.shape[1] * y0.shape[1] + x1.shape[1] * y1.shape[1]
            fan1 = x0.shape[1] * y1.shape[1] + x1.shape[1] * y0.shape[1]
            out0 = (jnp.einsum('eu,ev,uvw->ew', x0, y0, w000) + INV_SQRT3 * jnp.einsum('euk,evk,uvw->ew', x1, y1, w110)) / np.sqrt(fan0)
            out1 = (jnp.einsum('eu,evk,uvw->ewk', x0, y1, w011) + jnp.einsum('euk,ev,uvw->ewk', x1, y0, w101)) / np.sqrt(fan1)
            return (out0, out1)

        def _lin(x0, x1, w0, w1):
            return (x0 @ w0 / np.sqrt(x0.shape[1]), jnp.einsum('euk,uv->evk', x1, w1) / np.sqrt(x1.shape[1]))
        N = node_features.shape[0]
        row, col = (edge_index[0], edge_index[1])
        r_vec = edge_attr_tensor[:, :3]
        dist = edge_attr_tensor[:, 3:4]
        e0 = dist
        e1 = r_vec[:, None, :]
        xj0, xj1 = _split(node_features[col])
        m0, m1 = _tp(xj0, xj1, e0, e1, wm000, wm011, wm101, wm110)
        d0, d1 = _lin(xj0, xj1, lm0, lm1)
        msgs = _merge(m0 + d0, m1 + d1)
        agg = jax.ops.segment_sum(msgs, row, num_segments=N)
        a0, a1 = _split(agg)
        x0, x1 = _split(node_features)
        u0, u1 = _tp(x0, x1, a0, a1, wu000, wu011, wu101, wu110)
        ud0, ud1 = _lin(x0, x1, lu0, lu1)
        return node_features + _merge(u0 + ud0, u1 + ud1)

    def _L1_gnn_ref(node_features, edge_index, edge_attr_tensor, node_attr_scalar_raw, Wm_ss, Wm_vv, Wm_sv, Wm_vs, Lm_s, Lm_v, Wu_ss, Wu_vv, Wu_sv, Wu_vs, Lu_s, Lu_v):
        import jax, jax.numpy as jnp
        import numpy as np
        N = 2500
        E = 80000
        INV_SQRT3 = 0.5773502691896258
        INV8 = 0.125
        INV_SQRT32 = 0.17677669529663687
        INV64 = 0.015625
        INV32 = 0.03125
        INV_SQRT2048 = 0.022097086912079608
        n = node_features.shape[0]
        e = edge_attr_tensor.shape[0]
        row, col = (edge_index[0], edge_index[1])
        r_vec = edge_attr_tensor[:, :3]
        dist = edge_attr_tensor[:, 3:4]
        xj = node_features[col]
        s = xj[:, :64]
        v = xj[:, 64:].reshape(e, 32, 3)
        m0 = s @ Wm_ss * dist * INV8 + jnp.einsum('eui,ei->eu', v, r_vec) @ Wm_vv * (INV_SQRT3 * INV_SQRT32)
        m1 = (s @ Wm_sv)[:, :, None] * r_vec[:, None, :] * INV8 + jnp.einsum('eui,uw->ewi', v, Wm_vs) * dist[:, :, None] * INV_SQRT32
        m0 = m0 + s @ Lm_s * INV8
        m1 = m1 + jnp.einsum('eui,uw->ewi', v, Lm_v) * INV_SQRT32
        msg = jnp.concatenate([m0, m1.reshape(e, 96)], axis=-1)
        agg = jax.ops.segment_sum(msg, row, num_segments=n)
        a0 = agg[:, :64]
        a1 = agg[:, 64:].reshape(n, 32, 3)
        xs = node_features[:, :64]
        xv = node_features[:, 64:].reshape(n, 32, 3)
        u0 = jnp.einsum('nu,nv,uvw->nw', xs, a0, Wu_ss) * INV64 + jnp.einsum('nui,nvi,uvw->nw', xv, a1, Wu_vv) * (INV_SQRT3 * INV32)
        u1 = jnp.einsum('nu,nvi,uvw->nwi', xs, a1, Wu_sv) * INV_SQRT2048 + jnp.einsum('nui,nv,uvw->nwi', xv, a0, Wu_vs) * INV_SQRT2048
        u0 = u0 + xs @ Lu_s * INV8
        u1 = u1 + jnp.einsum('nui,uw->nwi', xv, Lu_v) * INV_SQRT32
        upd = jnp.concatenate([u0, u1.reshape(n, 96)], axis=-1)
        return node_features + upd
    edge_index = jnp.stack([src, dst])
    x = _layernorm(x + _L0_gnn_ref(x, edge_index, edge_attr_4, node_vec1, L0_gnn_wm000, L0_gnn_wm011, L0_gnn_wm101, L0_gnn_wm110, L0_gnn_lm0, L0_gnn_lm1, L0_gnn_wu000, L0_gnn_wu011, L0_gnn_wu101, L0_gnn_wu110, L0_gnn_lu0, L0_gnn_lu1), axis=-1)
    x = _layernorm(x + _L1_gnn_ref(x, edge_index, edge_attr_4, node_vec1, L1_gnn_Wm_ss, L1_gnn_Wm_vv, L1_gnn_Wm_sv, L1_gnn_Wm_vs, L1_gnn_Lm_s, L1_gnn_Lm_v, L1_gnn_Wu_ss, L1_gnn_Wu_vv, L1_gnn_Wu_sv, L1_gnn_Wu_vs, L1_gnn_Lu_s, L1_gnn_Lu_v), axis=-1)
    return x

_drawn_inputs = setup_inputs


def setup_inputs(seed=0):
    import zlib

    import numpy as np

    out = dict(_drawn_inputs(seed))
    spreads = {}
    factors = {}
    for name, (base, spread) in spreads.items():
        noise = np.random.default_rng([zlib.crc32(name.encode()), seed]).standard_normal(out[name].shape)
        drawn = base * np.exp(spread * noise) if base else spread * noise
        out[name] = jnp.asarray(drawn.astype(out[name].dtype))
    for name, factor in factors.items():
        out[name] = (out[name] * factor).astype(out[name].dtype)
    return out
```

```python
from contextlib import ExitStack

import concourse.bass as bass
import numpy as np
from concourse import mybir

ALU = mybir.AluOpType
ACT = mybir.ActivationFunctionType
AX_X = mybir.AxisListType.X
F32 = mybir.dt.float32
I32 = mybir.dt.int32
BF16 = mybir.dt.bfloat16

P = 128
S = 64
V = 32
D = S + 3 * V
TILE_NODES = 125
BLOCKS = 17
CAP = BLOCKS * P
REC = 8
COUNT_COLS = 4
COUNT_BUFS = 4
EPS = 1e-5

RAW, DIST, VR, RS = 0, D, 2 * D, 2 * D + V
FEAT = RS + 3 * S
HALF = 2 * D

SS = S * S
KV = 2 * V
MIX = V * KV
VV = V * V
QC = VV // P
ROUND = 1024
R0, R1 = SS // ROUND, MIX // ROUND
RS_ALL = R0 + R1
USES = R0 + 3 * R1


def used(r):
    return r + 1 if r < R0 else R0 + 3 * (r + 1 - R0)


class Named:
    pass


def layer_scales(layer):
    i3 = 1.0 / np.sqrt(3.0)
    if layer == 0:
        m, f0, f1 = 1.0 / np.sqrt(S + V), 1.0 / np.sqrt(S * S + V * V), 1.0 / np.sqrt(2 * S * V)
        return dict(m_ss=m, m_vv=i3 * m, m_sv=m, m_vs=m, l_s=S ** -0.5, l_v=V ** -0.5,
                    u_ss=f0, u_vv=i3 * f0, u_sv=f1, u_vs=f1)
    return dict(m_ss=S ** -0.5, m_vv=i3 * V ** -0.5, m_sv=S ** -0.5, m_vs=V ** -0.5,
                l_s=S ** -0.5, l_v=V ** -0.5, u_ss=1.0 / S, u_vv=i3 / V,
                u_sv=(S * V) ** -0.5, u_vs=(S * V) ** -0.5)


def build(nc, x, src, dst, attr, weights, out, tiles=None):
    N = x.shape[0]
    E = src.shape[0]
    NT = N // TILE_NODES
    assert NT * TILE_NODES == N and NT % 2 == 0
    COLS = -(-E // P)
    LAST = E - (P - 1) * COLS
    GROUP = COUNT_COLS * COUNT_BUFS
    STEPS = -(-COLS // GROUP)
    W = STEPS * GROUP
    SPILL0 = NT * CAP
    SLOTS = SPILL0 + COLS * P
    FILL = next(k for k in range(256, 0, -1) if SLOTS // P % k == 0)
    FILLS = SLOTS // P // FILL
    assert FILLS * FILL * P == SLOTS and 0 < LAST <= COLS and (COUNT_COLS + 1) * NT <= 512
    TRASH = N
    tiles = tiles or NT

    slots = nc.dram_tensor("slots", [SLOTS, REC], F32).ap()
    x_mid = nc.dram_tensor("x_mid", [N, D], F32).ap()
    ZROWS = -(-(N + P) // P) * P
    spill_sums = nc.dram_tensor("spill_sums", [ZROWS, FEAT], F32).ap()

    with ExitStack() as whole:
        def sb(name, shape, dt=F32, ctx=whole):
            return ctx.enter_context(nc.sbuf_tensor(name, shape, dt))

        def sem(name):
            return whole.enter_context(nc.semaphore(name))

        def bank(name, n=1):
            return whole.enter_context(nc.psum_tensor(name, [P, 512 * n], F32))

        sum_lo, sum_hi = bank("sum_lo"), bank("sum_hi")
        prods_ps = [bank("prods_ps0", 2), bank("prods_ps1", 2)]
        turn_ps = bank("turn_ps")
        small_ps = bank("small_ps")
        VRT = slice(2 * D, 2 * D + TILE_NODES)

        ident = sb("ident", [P, P])
        after = sb("after", [P, P])
        ones_f = sb("ones_f", [P, P])
        node_iota_i = sb("node_iota_i", [P, TILE_NODES], I32)
        node_iota = sb("node_iota", [P, TILE_NODES])
        eps_col = sb("eps_col", [P, 1])
        spill_blocks = sb("spill_blocks", [P, 1], I32)
        most = sb("most", [P, 1])
        trash_i = sb("trash_i", [P, 1], I32)
        trash = sb("trash", [P, 1])
        wt = []
        for layer in range(2):
            t = Named()
            t.bil = sb(f"w_bil{layer}", [P, SS + MIX])
            t.vv = sb(f"w_vv{layer}", [P, QC, S])
            t.msg0 = sb(f"w_msg0{layer}", [P, S])
            t.msg1 = sb(f"w_msg1{layer}", [P, V])
            t.msg_vr = sb(f"w_msg_vr{layer}", [V, S])
            t.lin0 = sb(f"w_lin0{layer}", [P, S])
            t.lin1 = sb(f"w_lin1{layer}", [3 * V, 3 * V])
            wt.append(t)

        early = ExitStack()
        so = Named()
        so.src_i = sb("src_i", [P, W], I32, early)
        so.dst_i = sb("dst_i", [P, W], I32, early)
        so.attr = sb("attr_sb", [P, W * 4], F32, early)
        so.src = sb("src_f", [P, W], F32, early)
        so.bucket_i = sb("bucket_i", [P, W], I32, early)
        so.bucket = sb("bucket", [P, W], F32, early)
        so.local = sb("local", [P, W], F32, early)
        so.tmp = sb("sort_tmp", [P, W], F32, early)
        so.base = sb("slot_base", [P, W], F32, early)
        so.spill_row = sb("spill_row", [P, 1], F32, early)
        so.spill_row_i = sb("spill_row_i", [P, 1], I32, early)
        so.ones_row = sb("ones_row", [P, COUNT_COLS], F32, early)
        so.spills = sb("spills", [P, COUNT_BUFS, COUNT_COLS], F32, early)
        so.iota_i = sb("bucket_iota_i", [P, NT], I32, early)
        so.iota = sb("bucket_iota", [P, NT], F32, early)
        so.empty = sb("empty_slots", [P, FILL, REC], F32, early)
        so.after = sb("after_bf", [P, P], BF16, early)
        so.ones = sb("ones_bf", [P, P], BF16, early)
        so.onehot = sb("bucket_onehot", [P, 2, COUNT_COLS + 1, NT], BF16, early)
        so.pick = sb("pick", [P, 2, COUNT_COLS, NT], F32, early)
        so.before = sb("before", [P, 2, NT], F32, early)
        so.rank = sb("rank", [P, COUNT_BUFS, COUNT_COLS], F32, early)
        so.place = sb("place", [P, COUNT_BUFS, 4, COUNT_COLS], F32, early)
        so.slot = sb("slot", [P, COUNT_BUFS, COUNT_COLS], I32, early)
        so.rec = sb("rec_out", [P, COUNT_BUFS, COUNT_COLS, REC], F32, early)
        early.close()

        recs = [sb(f"recs{b}", [P, BLOCKS, REC]) for b in range(2)]
        feat = [sb(f"feat{b}", [P, BLOCKS, FEAT]) for b in range(2)]
        onehot = [sb(f"onehot{b}", [P, BLOCKS, TILE_NODES]) for b in range(2)]
        xt = [sb(f"xt{b}", [P, D]) for b in range(2)]
        sums = sb("sums", [P, FEAT])
        sums_t = sb("sums_t", [P, 4 * TILE_NODES])
        vr_t = sb("vr_t", [V, TILE_NODES])
        ys = [sb(f"ys{b}", [P, 2 * S]) for b in range(2)]
        yv = [sb(f"yv{b}", [P, 3, KV]) for b in range(2)]
        yx = [sb(f"yx{b}", [P, 3 * V]) for b in range(2)]
        q3 = sb("q3", [P, 3 * VV])
        ys_t = sb("ys_t", [P, TILE_NODES])
        v_t = sb("v_t", [3 * V, TILE_NODES])
        work = sb("work", [P, 3 * ROUND])
        q = sb("q", [P, V * V])
        q_t = sb("q_t", [P, V * V // P, TILE_NODES])
        upd = sb("upd", [P, D])
        lin = sb("lin", [P, D])
        h = sb("h", [P, D])
        stats = sb("stats", [P, 8])
        sq = sb("sq", [P, D])
        res = [sb(f"res{b}", [P, D]) for b in range(2)]
        spill_in = [sb(f"spill_in{b}", [P, FEAT]) for b in range(2)]
        spill_rows = spill_in[0]
        spill_rec = sb("spill_rec", [P, REC])
        spill_key = sb("spill_key", [P, 8])
        spill_idx = sb("spill_idx", [P, 1], I32)
        spill_same = sb("spill_same", [P, 2, P])

        padded, edges_in, empty_made, emptied = sem("padded"), sem("edges_in"), sem("empty_made"), sem("emptied")
        iotas, consts, keyed, keys_ready = sem("iotas"), sem("consts"), sem("keyed"), sem("keys_ready")
        hot, counted, ranking, ranked, packed = sem("hot"), sem("counted"), sem("ranking"), sem("ranked"), sem("packed")
        scattered = [sem(f"scattered{b}") for b in range(COUNT_BUFS)]
        dma_go = sem("dma_go")
        sort_done, flag_ready, spills_turned = sem("sort_done"), sem("flag_ready"), sem("spills_turned")
        w_zeroed, w_in, w_ready = sem("w_zeroed"), sem("w_in"), sem("w_ready")

        HM = TILE_NODES

        def layer_sems(layer):
            s = {}
            for n in ("hot", "vr_mul", "vr", "scaled", "edges_done", "z_out", "turned", "turned_out", "agg",
                      "y_out", "y_turned", "y_turned_out", "prods", "prods_used", "upd", "q_mul", "q_add",
                      "q_ready", "q_turned", "q_turned_out", "lin", "lin_out", "h_part", "h_ready", "squares",
                      "deviation", "inverse", "normed",
                      "sp_rec", "sp_x", "sp_link", "sp_diag", "sp_keys", "sp_feat", "sp_sum", "sp_idx",
                      "sp_old", "sp_new", "sp_put", "sp_zero", "sp_zeroed", "sp_done"):
                s[n] = sem(f"{n}_l{layer}")
            for n in ("rec_in", "gathered", "x_in", "stored", "spill_in"):
                s[n] = [sem(f"{n}{b}_l{layer}") for b in range(2)]
            return s

        LS = [layer_sems(layer) for layer in range(2)]
        block = whole.enter_context(nc.Block())

        def sweep(eng, step):
            step(0, 0, 0, True, False)
            step(1, 0, 1, True, True)
            step(2, 1, 0, True, True)
            with eng.Fori(1, tiles // 2 - 1) as i:
                step(2 * i + 1, i, 1, True, True)
                step(2 * i + 2, i + 1, 0, True, True)
            step(tiles - 1, tiles // 2 - 1, 1, True, True)
            step(tiles, tiles // 2, 0, False, True)

        def at_least(t, n):
            return not isinstance(t, int) or t >= n

        @block.sync
        def _(sp):
            sp.wait_ge(padded, 3)
            for to, frm, w in ((so.src_i, src, 1), (so.dst_i, dst, 1), (so.attr, attr, 4)):
                full = (P - 1) * COLS * w
                sp.dma_start(to[0:P - 1, 0:COLS * w], frm[0:full].rearrange("(p c) -> p c", p=P - 1)).then_inc(edges_in, 16)
                sp.dma_start(to[P - 1:P, 0:LAST * w], frm[full:E * w].rearrange("(p c) -> p c", p=1)).then_inc(edges_in, 16)
            sp.wait_ge(empty_made, 2)
            slots_v = slots.rearrange("(p k) c -> p (k c)", p=P)
            for i in range(FILLS):
                sp.dma_start(slots_v[:, i * FILL * REC:(i + 1) * FILL * REC],
                             so.empty[:, :, :].rearrange("p k c -> p (k c)")).then_inc(emptied, 16)
            sp.wait_ge(w_zeroed, 1)
            for layer in range(2):
                w, t = weights[layer], wt[layer]
                mix = t.bil[:, SS:SS + MIX].rearrange("p (w k) -> p w k", k=KV)
                for to, frm in ((t.bil[S:P, 0:SS], w["u_ss"]), (mix[0:S, :, 0:V], w["u_sv"]), (mix[S:P, :, V:KV], w["u_vs"]),
                                (t.vv[:, :, :], w["u_vv"].rearrange("(c p) w -> p c w", p=P)),
                                (t.msg0[0:S, :], w["lm_s"]), (t.msg0[S:P, :], w["m_ss"]),
                                (t.msg1[0:S, :], w["m_sv"]), (t.msg1[S:S + V, :], w["lm_v"]), (t.msg1[S + V:P, :], w["m_vs"]),
                                (t.msg_vr[:, :], w["m_vv"]), (t.lin0[0:S, :], w["lu_s"])):
                    sp.dma_start(to, frm).then_inc(w_in, 16)
                for i in range(3):
                    sp.dma_start(t.lin1[V * i:V * i + V, V * i:V * i + V], w["lu_v"]).then_inc(w_in, 16)
            sp.wait_ge(sort_done, 1)
            sp.wait_ge(flag_ready, 1)
            n_spill = sp.value_load(spill_blocks[0:1, 0:1], min_val=0, max_val=COLS)

            for layer in range(2):
                s = LS[layer]
                table, to = (x, x_mid) if layer == 0 else (x_mid, out)
                if layer == 1:
                    for b in range(2):
                        sp.wait_ge(LS[0]["stored"][b], 16 * (tiles // 2))
                with sp.If(n_spill > 0):
                    sp.wait_ge(s["sp_zero"], 1)
                    zero = feat[0][:, :, :].rearrange("p k c -> p (k c)")
                    rows = spill_sums.rearrange("(p k) c -> p (k c)", p=P)
                    width, piece, n = ZROWS // P * FEAT, BLOCKS * FEAT, 0
                    for a in range(0, width, piece):
                        z = min(piece, width - a)
                        sp.dma_start(rows[:, a:a + z], zero[:, 0:z]).then_inc(s["sp_zeroed"], 16)
                    with sp.Fori(0, n_spill) as k:
                        sp.wait_ge(s["sp_put"], k * 16)
                        sp.dma_start(spill_rec[:, :], slots[bass.ds(k * P + SPILL0, P), :]).then_inc(s["sp_rec"], 16)
                sp.wait_ge(s["sp_done"], 1)

                def step(t, half, b, edges, nodes, s=s, table=table, to=to):
                    if edges:
                        if at_least(t, 2):
                            sp.wait_ge(s["edges_done"], t - 1)
                        sp.dma_start(recs[b][:, :, :], slots[bass.ds(t * CAP, CAP), :].rearrange("(p k) c -> p k c", k=BLOCKS)
                                     ).then_inc(s["rec_in"][b], 16)
                        with sp.If(n_spill > 0):
                            sp.dma_start(spill_in[b][0:HM, :], spill_sums[bass.ds(t * HM, HM), :]).then_inc(s["spill_in"][b], 16)
                    if at_least(t, 3):
                        sp.wait_ge(s["normed"], t - 2)
                        sp.dma_start(to[bass.ds((t - 3) * HM, HM), :], res[1 - b][0:HM, :]).then_inc(s["stored"][1 - b], 16)
                    if edges:
                        if at_least(t, 2):
                            sp.wait_ge(s["h_ready"], t - 1)
                            sp.wait_ge(s["q_mul"], t - 1)
                        sp.dma_start(xt[b][0:HM, :], table[bass.ds(t * HM, HM), :]).then_inc(s["x_in"][b], 16)

                sweep(sp, step)
                for t in (tiles - 2, tiles - 1):
                    sp.wait_ge(s["normed"], t + 1)
                    sp.dma_start(to[t * HM:(t + 1) * HM, :], res[t % 2][0:HM, :]).then_inc(s["stored"][t % 2], 16)
            for b in range(2):
                sp.wait_ge(LS[1]["stored"][b], 16 * (tiles // 2))

        @block.gpsimd
        def _(g):
            g.memset(so.src_i[:, :], N).then_inc(padded, 1)
            g.memset(so.dst_i[:, :], 0).then_inc(padded, 1)
            g.memset(so.attr[:, :], 0.0).then_inc(padded, 1)
            g.iota(so.iota_i[:, :], [[1, NT]], base=0, channel_multiplier=0).then_inc(iotas, 1)
            g.iota(so.spill_row_i[:, :], [[0, 1]], base=SPILL0 - P, channel_multiplier=1).then_inc(iotas, 1)
            g.iota(node_iota_i[:, :], [[1, TILE_NODES]], base=0, channel_multiplier=0).then_inc(iotas, 1)
            g.iota(trash_i[:, :], [[0, 1]], base=TRASH, channel_multiplier=1).then_inc(iotas, 1)
            g.memset(ones_f[:, :], 1.0).then_inc(iotas, 1)
            g.memset(so.ones[:, :], 1.0).then_inc(iotas, 1)
            g.wait_ge(iotas, 6)
            g.affine_select(so.after[:, :], so.ones[:, :], [[1, P]], ALU.is_gt, 0.0, base=0, channel_multiplier=-1).then_inc(iotas, 1)
            g.affine_select(after[:, :], ones_f[:, :], [[1, P]], ALU.is_gt, 0.0, base=0, channel_multiplier=-1).then_inc(iotas, 1)
            g.affine_select(ident[:, :], ones_f[:, :], [[1, P]], ALU.is_equal, 0.0, base=0, channel_multiplier=-1).then_inc(iotas, 1)
            last_slot = g.to_reg(SLOTS - 1)
            def carry():
                g.sem_inc(dma_go, 1)

            g.wait_ge(emptied, 16 * FILLS)
            with g.Fori(0, STEPS) as i:
                for b in range(COUNT_BUFS):
                    c = COUNT_BUFS * i + b
                    g.wait_ge(ranked, c + 1)
                    g.wait_ge(packed, 4 * c + 4)
                    carry()
                    for j in range(COUNT_COLS):
                        g.indirect_dma_start(out=slots[:, :], out_offset=bass.IndirectOffsetOnAxis(ap=so.slot[:, b, j:j + 1], axis=0),
                                             in_=so.rec[:, b, j, :], in_offset=None, bounds_check=last_slot, oob_is_err=False
                                             ).then_inc(scattered[b], 16)
            for b in range(COUNT_BUFS):
                g.wait_ge(scattered[b], 16 * COUNT_COLS * STEPS)
            g.nop().then_inc(sort_done, 1)
            g.wait_ge(flag_ready, 1)
            n_spill = g.value_load(spill_blocks[0:1, 0:1], min_val=0, max_val=COLS)

            for layer in range(2):
                s = LS[layer]
                table = x if layer == 0 else x_mid
                if layer == 1:
                    for b in range(2):
                        g.wait_ge(LS[0]["stored"][b], 16 * (tiles // 2))
                with g.If(n_spill > 0):
                    n_zero = -(-(ZROWS // P * FEAT) // (BLOCKS * FEAT))
                    g.wait_ge(s["sp_zeroed"], 16 * n_zero)
                    with g.Fori(0, n_spill) as k:
                        g.wait_ge(s["sp_rec"], 16 * k + 16)
                        carry()
                        g.indirect_dma_start(out=feat[1][:, 0, 0:D], out_offset=None, in_=table[:, :],
                                             in_offset=bass.IndirectOffsetOnAxis(ap=spill_rec[:, 0:1].bitcast(I32), axis=0)
                                             ).then_inc(s["sp_x"], 16)
                        g.wait_ge(s["sp_idx"], k + 1)
                        carry()
                        g.indirect_dma_start(out=spill_rows[:, :], out_offset=None, in_=spill_sums[:, :],
                                             in_offset=bass.IndirectOffsetOnAxis(ap=spill_idx[:, :], axis=0)
                                             ).then_inc(s["sp_old"], 16)
                        g.wait_ge(s["sp_new"], 2 * k + 2)
                        carry()
                        g.indirect_dma_start(out=spill_sums[:, :], out_offset=bass.IndirectOffsetOnAxis(ap=spill_idx[:, :], axis=0),
                                             in_=spill_rows[:, :], in_offset=None).then_inc(s["sp_put"], 16)
                    g.wait_ge(s["sp_put"], 16 * n_spill)
                g.nop().then_inc(s["sp_done"], 1)

                def gather(half, b, free, s=s, table=table):
                    if free is not None:
                        g.wait_ge(s["edges_done"], free)
                    g.wait_ge(s["rec_in"][b], 16 * half + 16)
                    carry()
                    for k in range(BLOCKS):
                        g.indirect_dma_start(out=feat[b][:, k, RAW:RAW + D], out_offset=None, in_=table[:, :],
                                             in_offset=bass.IndirectOffsetOnAxis(ap=recs[b][:, k, 0:1].bitcast(I32), axis=0)
                                             ).then_inc(s["gathered"][b], 16)

                def vector_products(n, nb, nh, s=s):
                    g.wait_ge(s["x_in"][nb], 16 * nh + 16)
                    g.wait_ge(s["y_out"], 4 * n + 4)
                    g.wait_ge(s["q_ready"], n)
                    g.tensor_tensor(q3[0:HM, :].rearrange("p (i u v) -> p i u v", i=3, u=V),
                                    xt[nb][0:HM, S:D].rearrange("p (u i) -> p i u", i=3).unsqueeze(3).broadcast_to([HM, 3, V, V]),
                                    yv[nb][0:HM, :, 0:V].unsqueeze(2).broadcast_to([HM, 3, V, V]), ALU.mult).then_inc(s["q_mul"], 1)

                gather(0, 0, None)
                gather(0, 1, None)
                with g.Fori(1, tiles // 2) as i:
                    vector_products(2 * i - 2, 0, i - 1)
                    gather(i, 0, 2 * i - 1)
                    vector_products(2 * i - 1, 1, i - 1)
                    gather(i, 1, 2 * i)
                vector_products(tiles - 2, 0, tiles // 2 - 1)
                vector_products(tiles - 1, 1, tiles // 2 - 1)

        @block.vector
        def _(ve):
            ve.memset(so.empty[:, :, :], 0.0).then_inc(empty_made, 1)
            ve.wait_ge(empty_made, 1)
            ve.memset(so.empty[:, :, 1:2], -1.0).then_inc(empty_made, 1)
            for layer in range(2):
                for z in (wt[layer].bil[:, :], wt[layer].lin0[:, :], wt[layer].lin1[:, :]):
                    last = ve.memset(z, 0.0)
            last.then_inc(w_zeroed, 1)
            ve.memset(eps_col[:, :], EPS)
            ve.memset(so.onehot[:, :, :, :], 0.0)
            ve.memset(so.before[:, :, :], 0.0)
            ve.memset(so.spills[:, :, :], 0.0)
            ve.memset(so.ones_row[:, :], 1.0)
            ve.memset(so.rec[:, :, :, :], 0.0).then_inc(consts, 1)
            ve.wait_ge(iotas, 4)
            ve.tensor_copy(so.iota[:, :], so.iota_i[:, :])
            ve.tensor_copy(trash[:, :], trash_i[:, :])
            ve.tensor_copy(node_iota[:, :], node_iota_i[:, :]).then_inc(consts, 1)
            ve.wait_ge(edges_in, 16 * 6)
            n = 0

            def chain(ins):
                nonlocal n
                n += 1
                ins.then_inc(keyed, 1)
                ve.wait_ge(keyed, n)

            bk, lo, tmp = so.bucket[:, :], so.local[:, :], so.tmp[:, :]
            chain(ve.tensor_copy(so.src[:, :], so.src_i[:, :]))
            chain(ve.tensor_scalar(tmp, so.src[:, :], 0.5, 1.0 / TILE_NODES, ALU.add, ALU.mult))
            chain(ve.tensor_scalar(so.bucket_i[:, :], tmp, -0.5, None, ALU.add))
            chain(ve.tensor_copy(bk, so.bucket_i[:, :]))
            chain(ve.scalar_tensor_tensor(lo, bk, -float(TILE_NODES), so.src[:, :], ALU.mult, ALU.add))
            chain(ve.tensor_scalar(tmp, lo, 0.0, None, ALU.is_lt))
            chain(ve.tensor_tensor(bk, bk, tmp, ALU.subtract))
            chain(ve.tensor_scalar(tmp, lo, float(TILE_NODES), None, ALU.is_ge))
            chain(ve.tensor_tensor(bk, bk, tmp, ALU.add))
            chain(ve.scalar_tensor_tensor(lo, bk, -float(TILE_NODES), so.src[:, :], ALU.mult, ALU.add))
            chain(ve.tensor_copy(so.spill_row[:, :], so.spill_row_i[:, :]))
            chain(ve.tensor_scalar(tmp, bk, float(NT), float(1 << 20), ALU.is_ge, ALU.mult))
            chain(ve.scalar_tensor_tensor(so.base[:, :], bk, float(CAP), tmp, ALU.mult, ALU.add))
            ve.nop().then_inc(keys_ready, 1)
            with ve.Fori(0, STEPS) as i:
                for b in range(COUNT_BUFS):
                    c = COUNT_BUFS * i + b
                    o, pb = c * COUNT_COLS, b % 2
                    m = 0
                    hots = so.onehot[:, pb, 0:COUNT_COLS, :]
                    cnt = (sum_lo, sum_hi)[pb][:, 0:(COUNT_COLS + 1) * NT].rearrange("p (j b) -> p j b", b=NT)
                    ve.tensor_tensor(hots, so.bucket[:, bass.ds(o, COUNT_COLS)].unsqueeze(2).broadcast_to([P, COUNT_COLS, NT]),
                                     so.iota[:, :].unsqueeze(1).broadcast_to([P, COUNT_COLS, NT]), ALU.is_equal).then_inc(hot, 1)
                    ve.wait_ge(counted, c + 1)

                    def link(ins):
                        nonlocal m
                        m += 1
                        ins.then_inc(ranking, 1)
                        ve.wait_ge(ranking, 10 * c + m)

                    pick, rank = so.pick[:, pb, :, :], so.rank[:, b, :]
                    pl = [so.place[:, b, k, :] for k in range(4)]
                    link(ve.tensor_tensor(so.before[:, 1 - pb, :], so.before[:, pb, :], cnt[:, COUNT_COLS, :], ALU.add))
                    link(ve.tensor_tensor(pick, cnt[:, 0:COUNT_COLS, :],
                                          so.before[:, pb, :].unsqueeze(1).broadcast_to([P, COUNT_COLS, NT]), ALU.add))
                    link(ve.tensor_tensor(pick, pick, hots, ALU.mult))
                    link(ve.tensor_reduce(rank, pick, AX_X, ALU.add))
                    link(ve.tensor_scalar(pl[0], rank, float(CAP), None, ALU.is_ge))
                    so_far = so.spills[:, b, :]
                    link(ve.tensor_tensor_scan(so_far, so.ones_row[:, :], pl[0], so.spills[:, (b - 1) % COUNT_BUFS, COUNT_COLS - 1:COUNT_COLS], ALU.mult, ALU.add))
                    link(ve.tensor_tensor(pl[1], so.base[:, bass.ds(o, COUNT_COLS)], rank, ALU.add))
                    link(ve.tensor_scalar(pl[2], so_far, float(P), so.spill_row[:, :], ALU.mult, ALU.add))
                    link(ve.tensor_tensor(pl[2], pl[2], pl[1], ALU.subtract))
                    link(ve.tensor_tensor(pl[3], pl[0], pl[2], ALU.mult))
                    ve.wait_ge(scattered[b], 16 * COUNT_COLS * i)
                    ve.tensor_tensor(so.slot[:, b, :], pl[1], pl[3], ALU.add).then_inc(ranked, 1)
            ve.wait_ge(spills_turned, 1)
            ve.tensor_reduce(most[0:1, :], small_ps[0:1, 0:P], AX_X, ALU.max).then_inc(keyed, 1)
            ve.wait_ge(keyed, n + 1)
            ve.tensor_copy(spill_blocks[0:1, :], most[0:1, :]).then_inc(flag_ready, 1)

            ve.wait_ge(w_in, 16 * 14 * 2)
            for layer in range(2):
                k, t = layer_scales(layer), wt[layer]
                mix = t.bil[:, SS:SS + MIX]
                for part, c in ((t.bil[S:P, 0:SS], "u_ss"), (mix[0:S, :], "u_sv"), (mix[S:P, :], "u_vs"),
                                (t.vv[:, :, :], "u_vv"), (t.msg0[0:S, :], "l_s"), (t.msg0[S:P, :], "m_ss"),
                                (t.msg1[0:S, :], "m_sv"), (t.msg1[S:S + V, :], "l_v"), (t.msg1[S + V:P, :], "m_vs"),
                                (t.msg_vr[:, :], "m_vv"), (t.lin0[0:S, :], "l_s"), (t.lin1[:, :], "l_v")):
                    last = ve.tensor_scalar(part, part, float(k[c]), None, ALU.mult)
            last.then_inc(w_ready, 1)
            ve.wait_ge(w_ready, 1)
            ve.wait_ge(flag_ready, 1)
            n_spill = ve.value_load(spill_blocks[0:1, 0:1], min_val=0, max_val=COLS)

            for layer in range(2):
                s = LS[layer]
                SPILL_LINKS = 16
                with ve.If(n_spill > 0):
                    if layer == 1:
                        ve.wait_ge(LS[0]["edges_done"], tiles)
                    else:
                        ve.wait_ge(sort_done, 1)
                    ve.memset(feat[0][:, :, :], 0.0).then_inc(s["sp_zero"], 1)
                    with ve.Fori(0, n_spill) as k:
                        m = 0

                        def link(ins, s=s, k=k):
                            nonlocal m
                            m += 1
                            ins.then_inc(s["sp_link"], 1)
                            ve.wait_ge(s["sp_link"], SPILL_LINKS * k + m)

                        f = feat[1][:, 0, :]
                        key, c8 = spill_rec[:, 6:7], [spill_key[:, j:j + 1] for j in range(8)]
                        ve.wait_ge(s["sp_rec"], 16 * k + 16)
                        link(ve.tensor_scalar(c8[0], spill_rec[:, 1:2], 0.0, None, ALU.is_ge))
                        link(ve.tensor_scalar(c8[1], c8[0], 1.0, None, ALU.subtract))
                        link(ve.scalar_tensor_tensor(c8[2], key, c8[0], c8[1], ALU.mult, ALU.add))
                        ve.tensor_scalar(spill_same[:, 0, :], ident[:, :], c8[2], None, ALU.mult).then_inc(s["sp_diag"], 1)
                        ve.wait_ge(s["sp_keys"], k + 1)
                        link(ve.tensor_scalar(spill_same[:, 1, :], small_ps[:, 0:P], c8[2], None, ALU.is_equal))
                        link(ve.tensor_tensor(spill_same[:, 0, :], spill_same[:, 1, :], after[:, :], ALU.mult))
                        link(ve.tensor_reduce(c8[3], spill_same[:, 0, :], AX_X, ALU.add))
                        link(ve.tensor_scalar(c8[4], c8[3], 0.0, None, ALU.is_equal))
                        link(ve.tensor_tensor(c8[4], c8[4], c8[0], ALU.mult))
                        link(ve.tensor_tensor(c8[5], key, trash[:, :], ALU.subtract))
                        link(ve.tensor_tensor(c8[6], c8[5], c8[4], ALU.mult))
                        ve.tensor_tensor(spill_idx[:, :], c8[6], trash[:, :], ALU.add).then_inc(s["sp_idx"], 1)
                        ve.wait_ge(s["sp_x"], 16 * k + 16)
                        vec = f[:, S:D].rearrange("p (u i) -> p u i", i=3)
                        link(ve.tensor_scalar(f[:, DIST:DIST + D], f[:, 0:D], spill_rec[:, 5:6], None, ALU.mult))
                        link(ve.tensor_scalar(f[:, VR:VR + V], vec[:, :, 0], spill_rec[:, 2:3], None, ALU.mult))
                        link(ve.scalar_tensor_tensor(f[:, VR:VR + V], vec[:, :, 1], spill_rec[:, 3:4], f[:, VR:VR + V], ALU.mult, ALU.add))
                        link(ve.scalar_tensor_tensor(f[:, VR:VR + V], vec[:, :, 2], spill_rec[:, 4:5], f[:, VR:VR + V], ALU.mult, ALU.add))
                        for i in range(3):
                            rs = ve.tensor_scalar(f[:, RS + S * i:RS + S * i + S], f[:, 0:S], spill_rec[:, 2 + i:3 + i], None, ALU.mult)
                            if i < 2:
                                link(rs)
                        rs.then_inc(s["sp_feat"], 1)
                        assert m == SPILL_LINKS
                        ve.wait_ge(s["sp_sum"], k + 1)
                        ve.wait_ge(s["sp_old"], 16 * k + 16)
                        ve.tensor_tensor(spill_rows[:, 0:HALF], spill_rows[:, 0:HALF], sum_lo[:, 0:HALF], ALU.add).then_inc(s["sp_new"], 1)
                        ve.tensor_tensor(spill_rows[:, HALF:FEAT], spill_rows[:, HALF:FEAT], sum_hi[:, 0:FEAT - HALF], ALU.add).then_inc(s["sp_new"], 1)
                ve.wait_ge(s["sp_done"], 1)

                def step(t, half, b, edges, nodes, s=s):
                    if edges:
                        ve.wait_ge(s["rec_in"][b], 16 * half + 16)
                        if at_least(t, 2):
                            ve.wait_ge(s["edges_done"], t - 1)
                        ve.tensor_tensor(onehot[b][:, :, :], recs[b][:, :, 1:2].broadcast_to([P, BLOCKS, HM]),
                                         node_iota[:, :].unsqueeze(1).broadcast_to([P, BLOCKS, HM]), ALU.is_equal).then_inc(s["hot"], 1)
                        ve.wait_ge(s["gathered"][b], 16 * BLOCKS * half + 16 * BLOCKS)
                        if at_least(t, 2):
                            ve.wait_ge(s["upd"], RS_ALL * (t - 1))
                        elif at_least(t, 1):
                            ve.wait_ge(s["vr"], t)
                        vr = work[:, 0:BLOCKS * 3 * V].rearrange("p (k u i) -> p k u i", u=V, i=3)
                        ve.tensor_tensor(vr, feat[b][:, :, S:D].rearrange("p k (u i) -> p k u i", i=3),
                                         recs[b][:, :, 2:5].unsqueeze(2).broadcast_to([P, BLOCKS, V, 3]), ALU.mult).then_inc(s["vr_mul"], 1)
                        ve.wait_ge(s["vr_mul"], t + 1)
                        ve.tensor_reduce(feat[b][:, :, VR:VR + V], vr, AX_X, ALU.add).then_inc(s["vr"], 1)
                    if not nodes:
                        return
                    n, nb, nh = t - 1, 1 - b, (half if b == 1 else half - 1)
                    X = xt[nb][0:HM, :]
                    ve.wait_ge(s["x_in"][nb], 16 * nh + 16)
                    ve.wait_ge(s["q_mul"], n + 1)
                    ve.wait_ge(s["q_turned"], 2 * n)
                    ve.tensor_tensor(q[0:HM, :], q3[0:HM, 0:VV], q3[0:HM, VV:2 * VV], ALU.add).then_inc(s["q_add"], 1)
                    ve.wait_ge(s["q_add"], n + 1)
                    ve.tensor_tensor(q[0:HM, :], q[0:HM, :], q3[0:HM, 2 * VV:3 * VV], ALU.add).then_inc(s["q_ready"], 1)
                    if at_least(t, 2):
                        normalise(t - 2, half - 1, b, s)
                    if edges:
                        ve.wait_ge(s["vr"], t + 1)
                    else:
                        ve.wait_ge(s["upd"], RS_ALL * n)
                    ve.wait_ge(s["h_part"], 3 * n)
                    ve.wait_ge(s["y_out"], 4 * n + 4)
                    for r in range(R0):
                        ve.wait_ge(s["prods"], RS_ALL * n + r + 1)
                        if r >= 2:
                            ve.wait_ge(s["upd"], RS_ALL * n + r - 1)
                        wk = work[0:HM, ROUND * (r % 2):ROUND * (r % 2) + ROUND].rearrange("p (w u) -> p w u", u=S)
                        ve.tensor_tensor(wk, prods_ps[r % 2][0:HM, :].rearrange("p (w u) -> p w u", u=S),
                                         X[:, 0:S].unsqueeze(1).broadcast_to([HM, ROUND // S, S]), ALU.mult).then_inc(s["prods_used"], 1)
                        ve.wait_ge(s["prods_used"], USES * n + used(r))
                        ve.tensor_reduce(upd[0:HM, ROUND // S * r:ROUND // S * (r + 1)], wk, AX_X, ALU.add).then_inc(s["upd"], 1)
                    wk = work[0:HM, :].rearrange("p (i w k) -> p i w k", i=3, k=KV)
                    upd1 = upd[0:HM, S:D].rearrange("p (w i) -> p i w", i=3)
                    for r in range(R0, R0 + R1):
                        ve.wait_ge(s["prods"], RS_ALL * n + r + 1)
                        ve.wait_ge(s["upd"], RS_ALL * n + r)
                        for i in range(3):
                            ve.tensor_tensor(wk[:, i, :, :], prods_ps[r % 2][0:HM, :].rearrange("p (w k) -> p w k", k=KV),
                                             yv[nb][0:HM, i, :].unsqueeze(1).broadcast_to([HM, ROUND // KV, KV]), ALU.mult).then_inc(s["prods_used"], 1)
                        ve.wait_ge(s["prods_used"], USES * n + used(r))
                        w0 = ROUND // KV * (r - R0)
                        ve.tensor_reduce(upd1[:, :, w0:w0 + ROUND // KV], wk, AX_X, ALU.add).then_inc(s["upd"], 1)
                    ve.wait_ge(s["lin_out"], 2 * n + 2)
                    ve.wait_ge(s["normed"], n)
                    ve.scalar_tensor_tensor(h[0:HM, :], X, 2.0, lin[0:HM, :], ALU.mult, ALU.add).then_inc(s["h_part"], 1)
                    ve.wait_ge(s["upd"], RS_ALL * n + RS_ALL)
                    ve.wait_ge(s["h_part"], 3 * n + 1)
                    ve.tensor_tensor(h[0:HM, :], h[0:HM, :], upd[0:HM, :], ALU.add).then_inc(s["h_part"], 1)
                    ve.wait_ge(s["h_part"], 3 * n + 2)
                    ve.tensor_reduce(stats[0:HM, 0:1], h[0:HM, :], AX_X, ALU.add).then_inc(s["h_part"], 1)
                    ve.wait_ge(s["h_part"], 3 * n + 3)
                    ve.tensor_scalar(stats[0:HM, 1:2], stats[0:HM, 0:1], -1.0 / D, None, ALU.mult).then_inc(s["h_ready"], 1)

                def normalise(n, half, b, s):
                    ve.wait_ge(s["deviation"], n + 1)
                    ve.wait_ge(s["stored"][b], 16 * half)
                    ve.reciprocal(stats[0:HM, 4:5], stats[0:HM, 3:4]).then_inc(s["inverse"], 1)
                    ve.wait_ge(s["inverse"], n + 1)
                    ve.tensor_scalar(res[b][0:HM, :], h[0:HM, :], stats[0:HM, 1:2], stats[0:HM, 4:5], ALU.add, ALU.mult
                                     ).then_inc(s["normed"], 1)

                sweep(ve, step)
                normalise(tiles - 1, tiles // 2 - 1, 1, s)

        @block.tensor
        def _(te):
            te.wait_ge(iotas, 9)
            te.wait_ge(consts, 1)
            with te.Fori(0, STEPS) as i:
                for b in range(COUNT_BUFS):
                    te.wait_ge(hot, COUNT_BUFS * i + b + 1)
                    cnt = (sum_lo, sum_hi)[b % 2][:, 0:(COUNT_COLS + 1) * NT]
                    hots = so.onehot[:, b % 2, :, :].rearrange("p j b -> p (j b)")
                    te.matmul(cnt, so.after[:, :], hots, start=True, stop=False)
                    for c in range(1, COUNT_COLS + 1):
                        mm = te.matmul(cnt[:, c * NT:], so.ones[:, :], hots[:, 0:(COUNT_COLS + 1 - c) * NT],
                                       start=False, stop=(c == COUNT_COLS))
                    mm.then_inc(counted, 1)
            te.wait_ge(ranked, COUNT_BUFS * STEPS)
            te.transpose(small_ps[0:1, 0:P], so.spills[:, COUNT_BUFS - 1, COUNT_COLS - 1:COUNT_COLS], ident[:, :]).then_inc(spills_turned, 1)
            te.wait_ge(w_ready, 1)
            te.wait_ge(flag_ready, 1)
            n_spill = te.value_load(spill_blocks[0:1, 0:1], min_val=0, max_val=COLS)
            for layer in range(2):
                s, w = LS[layer], wt[layer]
                with te.If(n_spill > 0):
                    with te.Fori(0, n_spill) as k:
                        te.wait_ge(s["sp_diag"], k + 1)
                        te.matmul(small_ps[:, 0:P], ones_f[:, :], spill_same[:, 0, :], start=True, stop=True).then_inc(s["sp_keys"], 1)
                        te.wait_ge(s["sp_feat"], k + 1)
                        te.matmul(sum_lo[:, 0:HALF], spill_same[:, 1, :], feat[1][:, 0, 0:HALF], start=True, stop=True)
                        te.matmul(sum_hi[:, 0:FEAT - HALF], spill_same[:, 1, :], feat[1][:, 0, HALF:FEAT],
                                  start=True, stop=True).then_inc(s["sp_sum"], 1)
                te.wait_ge(s["sp_done"], 1)

                def sum_edges(t, half, b, ks, s=s):
                    for k in ks:
                        if k == 0:
                            te.wait_ge(s["hot"], t + 1)
                            te.wait_ge(s["vr"], t + 1)
                        te.wait_ge(s["scaled"], BLOCKS * t + k + 1)
                        lhs = onehot[b][:, k, :]
                        te.matmul(sum_lo[0:HM, 0:HALF], lhs, feat[b][:, k, 0:HALF], start=(k == 0), stop=(k == BLOCKS - 1))
                        mm = te.matmul(sum_hi[0:HM, 0:FEAT - HALF], lhs, feat[b][:, k, HALF:FEAT], start=(k == 0), stop=(k == BLOCKS - 1))
                        if k == 0:
                            with te.If(n_spill > 0):
                                te.wait_ge(s["spill_in"][b], 16 * half + 16)
                                te.matmul(sum_lo[0:HM, 0:HALF], ident[0:HM, 0:HM], spill_in[b][0:HM, 0:HALF], start=False, stop=False)
                                te.matmul(sum_hi[0:HM, 0:FEAT - HALF], ident[0:HM, 0:HM], spill_in[b][0:HM, HALF:FEAT], start=False, stop=False)
                        if k == BLOCKS - 1:
                            mm.then_inc(s["edges_done"], 1)

                def step(t, half, b, edges, nodes, s=s, w=w):
                    cuts = [range(0, 6), range(6, 10), range(10, 14), range(14, BLOCKS)]
                    if not nodes:
                        for ks in cuts:
                            sum_edges(t, half, b, ks)
                        return
                    n = t - 1
                    nb = 1 - b
                    idn = ident[0:HM, 0:HM]

                    def turn_q(part):
                        for c in range(QC // 2):
                            mm = te.transpose(turn_ps[:, HM * c:HM * c + HM], q[0:HM, P * (c + part * QC // 2):P * (c + part * QC // 2 + 1)], idn)
                        mm.then_inc(s["q_turned"], 1)

                    def bilinear(r):
                        if r >= 2:
                            te.wait_ge(s["prods_used"], USES * n + used(r - 2))
                        elif at_least(n, 1) and at_least(t, 2):
                            te.wait_ge(s["prods_used"], USES * n - USES + used(r + RS_ALL - 2))
                        for hh in range(2):
                            c = ROUND * r + 512 * hh
                            rows = slice(S, P) if c < SS else slice(0, P)
                            mm = te.matmul(prods_ps[r % 2][0:HM, 512 * hh:512 * hh + 512], ys_t[rows, :], w.bil[rows, c:c + 512],
                                           start=True, stop=True)
                        mm.then_inc(s["prods"], 1)

                    te.wait_ge(s["z_out"], 4 * n + 4)
                    te.wait_ge(s["q_turned_out"], 2 * n)
                    for c in range(4):
                        te.transpose(turn_ps[:, HM * c:HM * c + HM], sums[0:HM, P * c:P * c + P], idn)
                    te.wait_ge(s["lin_out"], 2 * n)
                    te.transpose(small_ps[0:V, VRT], sums[0:HM, 4 * P:FEAT], idn).then_inc(s["turned"], 1)
                    te.wait_ge(s["turned_out"], 2 * n + 2)
                    te.matmul(small_ps[0:HM, D:D + S], sums_t[:, 0:HM], w.msg0[:, :], start=True, stop=False)
                    te.matmul(small_ps[0:HM, D:D + S], vr_t[:, :], w.msg_vr[:, :], start=False, stop=True)
                    for i in range(3):
                        mm = te.matmul(small_ps[0:HM, D + S + V * i:D + S + V * i + V], sums_t[:, HM * (i + 1):HM * (i + 2)], w.msg1[:, :],
                                       start=True, stop=True)
                    mm.then_inc(s["agg"], 1)
                    te.wait_ge(s["y_out"], 4 * n + 4)
                    te.transpose(turn_ps[:, 0:HM], ys[nb][0:HM, :], idn)
                    te.transpose(turn_ps[0:3 * V, HM:2 * HM], yx[nb][0:HM, :], idn).then_inc(s["y_turned"], 1)
                    te.wait_ge(s["y_turned_out"], 2 * n + 2)
                    bilinear(0)
                    bilinear(1)
                    te.wait_ge(s["q_ready"], n + 1)
                    turn_q(0)
                    if edges:
                        sum_edges(t, half, b, cuts[0])
                    bilinear(2)
                    if edges:
                        sum_edges(t, half, b, cuts[1])
                    bilinear(3)
                    te.wait_ge(s["q_turned_out"], 2 * n + 1)
                    turn_q(1)
                    if edges:
                        sum_edges(t, half, b, cuts[2])
                    bilinear(4)
                    te.wait_ge(s["q_turned_out"], 2 * n + 2)
                    te.matmul(small_ps[0:HM, S:D], v_t[:, :], w.lin1[:, :], start=True, stop=True)
                    te.matmul(small_ps[0:HM, 0:S], ys_t[:, :], w.lin0[:, :], start=True, stop=False)
                    for c in range(QC):
                        mm = te.matmul(small_ps[0:HM, 0:S], q_t[:, c, :], w.vv[:, c, :], start=False, stop=(c == QC - 1))
                    mm.then_inc(s["lin"], 1)
                    bilinear(5)
                    if edges:
                        sum_edges(t, half, b, cuts[3])

                sweep(te, step)

        @block.scalar
        def _(ac):
            ac.wait_ge(keys_ready, 1)
            with ac.Fori(0, STEPS) as i:
                for b in range(COUNT_BUFS):
                    o = (COUNT_BUFS * i + b) * COUNT_COLS
                    cols = bass.ds(o, COUNT_COLS)
                    ac.wait_ge(scattered[b], 16 * COUNT_COLS * i)
                    ac.copy(so.rec[:, b, :, 0:1].bitcast(I32), so.dst_i[:, cols].unsqueeze(2)).then_inc(packed, 1)
                    ac.copy(so.rec[:, b, :, 1:2], so.local[:, cols].unsqueeze(2)).then_inc(packed, 1)
                    ac.copy(so.rec[:, b, :, 2:6], so.attr[:, bass.ds(o * 4, COUNT_COLS * 4)].rearrange("p (j f) -> p j f", f=4)
                            ).then_inc(packed, 1)
                    ac.copy(so.rec[:, b, :, 6:7], so.src[:, cols].unsqueeze(2)).then_inc(packed, 1)
            for layer in range(2):
                s = LS[layer]

                def deviation(n, s=s):
                    ac.wait_ge(s["h_ready"], n + 1)
                    ac.activation(sq[0:HM, :], h[0:HM, :], ACT.Square, bias=stats[0:HM, 1:2], accum_out=stats[0:HM, 2:3]).then_inc(s["squares"], 1)
                    ac.wait_ge(s["squares"], n + 1)
                    ac.activation(stats[0:HM, 3:4], stats[0:HM, 2:3], ACT.Sqrt, bias=eps_col[0:HM, :], scale=1.0 / D).then_inc(s["deviation"], 1)

                def scale_edges(t, half, b, ks, s=s):
                    for k in ks:
                        if k == 0:
                            ac.wait_ge(s["gathered"][b], 16 * BLOCKS * half + 16 * BLOCKS)
                        f = feat[b][:, k, :]
                        ac.activation(f[:, DIST:DIST + D], f[:, RAW:RAW + D], ACT.Copy, scale=recs[b][:, k, 5:6])
                        for i in range(3):
                            last = ac.activation(f[:, RS + S * i:RS + S * i + S], f[:, RAW:RAW + S], ACT.Copy, scale=recs[b][:, k, 2 + i:3 + i])
                        last.then_inc(s["scaled"], 1)

                def step(t, half, b, edges, nodes, s=s):
                    cuts = [range(0, 6), range(6, 12), range(12, BLOCKS)]
                    if not nodes:
                        for ks in cuts:
                            scale_edges(t, half, b, ks)
                        return
                    n, nb, nh = t - 1, 1 - b, (half if b == 1 else half - 1)
                    ac.wait_ge(s["x_in"][nb], 16 * nh + 16)
                    if at_least(t, 3):
                        ac.wait_ge(s["y_turned"], n - 1)
                        ac.wait_ge(s["prods_used"], USES * (n - 1))
                        ac.wait_ge(s["q_mul"], n - 1)
                    xv = xt[nb][0:HM, S:D].rearrange("p (u i) -> p i u", i=3)
                    ac.copy(ys[nb][0:HM, 0:S], xt[nb][0:HM, 0:S]).then_inc(s["y_out"], 1)
                    ac.copy(yx[nb][0:HM, :].rearrange("p (i u) -> p i u", i=3), xv)
                    ac.copy(yv[nb][0:HM, :, V:KV], xv).then_inc(s["y_out"], 1)
                    ac.wait_ge(s["edges_done"], n + 1)
                    lo = sum_lo[0:HM, 0:HALF].rearrange("p (c f) -> p c f", c=2)
                    groups = sums[0:HM, P:4 * P].rearrange("p (i f) -> p i f", i=3)
                    ac.copy(sums[0:HM, 0:P].rearrange("p (c f) -> p c f", c=2), lo[:, :, 0:S]).then_inc(s["z_out"], 1)
                    ac.copy(groups[:, :, S:P].rearrange("p i (c u) -> p i c u", c=2),
                            lo[:, :, S:D].rearrange("p c (u i) -> p i c u", i=3)).then_inc(s["z_out"], 1)
                    ac.copy(groups[:, :, 0:S], sum_hi[0:HM, V:V + 3 * S].rearrange("p (i f) -> p i f", i=3)).then_inc(s["z_out"], 1)
                    ac.copy(sums[0:HM, 4 * P:FEAT], sum_hi[0:HM, 0:V]).then_inc(s["z_out"], 1)
                    ac.wait_ge(s["turned"], n + 1)
                    ac.copy(sums_t[:, :], turn_ps[:, 0:4 * HM]).then_inc(s["turned_out"], 1)
                    ac.copy(vr_t[:, :], small_ps[0:V, VRT]).then_inc(s["turned_out"], 1)
                    ac.wait_ge(s["agg"], n + 1)
                    ac.copy(ys[nb][0:HM, S:2 * S], small_ps[0:HM, D:D + S]).then_inc(s["y_out"], 1)
                    ac.copy(yv[nb][0:HM, :, 0:V], small_ps[0:HM, D + S:2 * D].rearrange("p (i u) -> p i u", i=3)).then_inc(s["y_out"], 1)
                    ac.wait_ge(s["y_turned"], n + 1)
                    ac.copy(ys_t[:, :], turn_ps[:, 0:HM]).then_inc(s["y_turned_out"], 1)
                    ac.copy(v_t[:, :], turn_ps[0:3 * V, HM:2 * HM]).then_inc(s["y_turned_out"], 1)
                    if at_least(t, 2):
                        deviation(t - 2)
                    for part in range(2):
                        if edges:
                            scale_edges(t, half, b, cuts[part])
                        ac.wait_ge(s["q_turned"], 2 * n + part + 1)
                        ac.copy(q_t[:, QC // 2 * part:QC // 2 * (part + 1), :], turn_ps[:, 0:QC // 2 * HM].rearrange("p (c n) -> p c n", n=HM)
                                ).then_inc(s["q_turned_out"], 1)
                    if edges:
                        scale_edges(t, half, b, cuts[2])
                    ac.wait_ge(s["lin"], n + 1)
                    ac.wait_ge(s["h_part"], 3 * n)
                    ac.copy(lin[0:HM, 0:S], small_ps[0:HM, 0:S]).then_inc(s["lin_out"], 1)
                    ac.copy(lin[0:HM, S:D].rearrange("p (u i) -> p u i", i=3),
                            small_ps[0:HM, S:D].rearrange("p (i u) -> p u i", i=3)).then_inc(s["lin_out"], 1)

                sweep(ac, step)
                deviation(tiles - 1)


_WEIGHTS = {
    "m_ss": ("L0_gnn_wm000", "L1_gnn_Wm_ss"), "m_vv": ("L0_gnn_wm110", "L1_gnn_Wm_vv"),
    "m_sv": ("L0_gnn_wm011", "L1_gnn_Wm_sv"), "m_vs": ("L0_gnn_wm101", "L1_gnn_Wm_vs"),
    "lm_s": ("L0_gnn_lm0", "L1_gnn_Lm_s"), "lm_v": ("L0_gnn_lm1", "L1_gnn_Lm_v"),
    "lu_s": ("L0_gnn_lu0", "L1_gnn_Lu_s"), "lu_v": ("L0_gnn_lu1", "L1_gnn_Lu_v"),
    "u_ss": ("L0_gnn_wu000", "L1_gnn_Wu_ss"), "u_sv": ("L0_gnn_wu011", "L1_gnn_Wu_sv"),
    "u_vs": ("L0_gnn_wu101", "L1_gnn_Wu_vs"), "u_vv": ("L0_gnn_wu110", "L1_gnn_Wu_vv"),
}


def laid_out(name, a):
    if name in ("u_ss", "u_vs"):
        a = a.transpose(1, 2, 0)
        return np.ascontiguousarray(a.reshape(S, SS) if name == "u_ss" else a)
    if name == "u_sv":
        return np.ascontiguousarray(a.transpose(0, 2, 1))
    if name == "u_vv":
        return np.ascontiguousarray(a.reshape(V * V, S))
    return np.ascontiguousarray(a.reshape(-1, a.shape[-1]))


def kernel(**inputs):
    import concourse.bacc as bacc
    from concourse.bass_utils import run_bass_kernel_spmd

    nc = bacc.Bacc("TRN2", target_bir_lowering=False, num_devices=1)
    arrays = {}

    def given(name, a):
        arrays[name] = a
        return nc.dram_tensor(name, a.shape, mybir.dt.from_np(a.dtype), kind="ExternalInput").ap()

    x = given("x", np.ascontiguousarray(inputs["x"]))
    src = given("src", np.ascontiguousarray(inputs["src"]))
    dst = given("dst", np.ascontiguousarray(inputs["dst"]))
    attr = given("edge_attr", np.ascontiguousarray(inputs["edge_attr_4"]).reshape(-1))
    weights = [{k: given(f"{k}_{layer}", laid_out(k, np.asarray(inputs[names[layer]])))
                for k, names in _WEIGHTS.items()} for layer in range(2)]
    out = nc.dram_tensor("out", inputs["x"].shape, F32, kind="ExternalOutput").ap()
    build(nc, x, src, dst, attr, weights, out)
    r = run_bass_kernel_spmd(nc, [arrays], core_ids=[0])
    return r.results[0]["out"]
```

```python
from contextlib import ExitStack

import concourse.bass as bass
import numpy as np
from concourse import mybir

ALU = mybir.AluOpType
ACT = mybir.ActivationFunctionType
AX_X = mybir.AxisListType.X
F32 = mybir.dt.float32
I32 = mybir.dt.int32
BF16 = mybir.dt.bfloat16

P = 128
S = 64
V = 32
D = S + 3 * V
TILE_NODES = 125
BLOCKS = 17
CAP = BLOCKS * P
REC = 8
SPLIT = 9
COUNT_COLS = 4
COUNT_BUFS = 4
EPS = 1e-5

RAW, DIST, VR, RS = 0, D, 2 * D, 2 * D + V
FEAT = RS + 3 * S
HALF = 2 * D

SS = S * S
KV = 2 * V
MIX = V * KV
VV = V * V
QC = VV // P
ROUND = 1024
R0, R1 = SS // ROUND, MIX // ROUND
RS_ALL = R0 + R1
USES = R0 + 3 * R1


def used(r):
    return r + 1 if r < R0 else R0 + 3 * (r + 1 - R0)


class Named:
    pass


def layer_scales(layer):
    i3 = 1.0 / np.sqrt(3.0)
    if layer == 0:
        m, f0, f1 = 1.0 / np.sqrt(S + V), 1.0 / np.sqrt(S * S + V * V), 1.0 / np.sqrt(2 * S * V)
        return dict(m_ss=m, m_vv=i3 * m, m_sv=m, m_vs=m, l_s=S ** -0.5, l_v=V ** -0.5,
                    u_ss=f0, u_vv=i3 * f0, u_sv=f1, u_vs=f1)
    return dict(m_ss=S ** -0.5, m_vv=i3 * V ** -0.5, m_sv=S ** -0.5, m_vs=V ** -0.5,
                l_s=S ** -0.5, l_v=V ** -0.5, u_ss=1.0 / S, u_vv=i3 / V,
                u_sv=(S * V) ** -0.5, u_vs=(S * V) ** -0.5)


def build(nc, x, src, dst, attr, weights, out, tiles=None):
    N = x.shape[0]
    E = src.shape[0]
    NT = N // TILE_NODES
    assert NT * TILE_NODES == N and NT % 2 == 0
    COLS = -(-E // P)
    LAST = E - (P - 1) * COLS
    GROUP = COUNT_COLS * COUNT_BUFS
    STEPS = -(-COLS // GROUP)
    W = STEPS * GROUP
    SPILL0 = NT * CAP
    SLOTS = SPILL0 + COLS * P
    FILL = next(k for k in range(256, 0, -1) if SLOTS // P % k == 0)
    FILLS = SLOTS // P // FILL
    assert FILLS * FILL * P == SLOTS and 0 < LAST <= COLS and (COUNT_COLS + 1) * NT <= 512
    TRASH = N
    tiles = tiles or NT

    slots = nc.dram_tensor("slots", [SLOTS, REC], F32).ap()
    x_mid = nc.dram_tensor("x_mid", [N, D], F32).ap()
    ZROWS = -(-(N + P) // P) * P
    spill_sums = nc.dram_tensor("spill_sums", [ZROWS, FEAT], F32).ap()

    with ExitStack() as whole:
        def sb(name, shape, dt=F32, ctx=whole):
            return ctx.enter_context(nc.sbuf_tensor(name, shape, dt))

        def sem(name):
            return whole.enter_context(nc.semaphore(name))

        def bank(name, n=1):
            return whole.enter_context(nc.psum_tensor(name, [P, 512 * n], F32))

        sum_lo, sum_hi = bank("sum_lo"), bank("sum_hi")
        prods_ps = [bank("prods_ps0", 2), bank("prods_ps1", 2)]
        turn_ps = bank("turn_ps")
        small_ps = bank("small_ps")
        VRT = slice(2 * D, 2 * D + TILE_NODES)

        ident = sb("ident", [P, P])
        after = sb("after", [P, P])
        ones_f = sb("ones_f", [P, P])
        node_iota_i = sb("node_iota_i", [P, TILE_NODES], I32)
        node_iota = sb("node_iota", [P, TILE_NODES])
        eps_col = sb("eps_col", [P, 1])
        spill_blocks = sb("spill_blocks", [P, 1], I32)
        most = sb("most", [P, 1])
        trash_i = sb("trash_i", [P, 1], I32)
        trash = sb("trash", [P, 1])
        wt = []
        for layer in range(2):
            t = Named()
            t.bil = sb(f"w_bil{layer}", [P, SS + MIX])
            t.vv = sb(f"w_vv{layer}", [P, QC, S])
            t.msg0 = sb(f"w_msg0{layer}", [P, S])
            t.msg1 = sb(f"w_msg1{layer}", [P, V])
            t.msg_vr = sb(f"w_msg_vr{layer}", [V, S])
            t.lin0 = sb(f"w_lin0{layer}", [P, S])
            t.lin1 = sb(f"w_lin1{layer}", [3 * V, 3 * V])
            wt.append(t)

        early = ExitStack()
        so = Named()
        so.src_i = sb("src_i", [P, W], I32, early)
        so.dst_i = sb("dst_i", [P, W], I32, early)
        so.attr = sb("attr_sb", [P, W * 4], F32, early)
        so.src = sb("src_f", [P, W], F32, early)
        so.bucket_i = sb("bucket_i", [P, W], I32, early)
        so.bucket = sb("bucket", [P, W], F32, early)
        so.local = sb("local", [P, W], F32, early)
        so.tmp = sb("sort_tmp", [P, W], F32, early)
        so.base = sb("slot_base", [P, W], F32, early)
        so.spill_row = sb("spill_row", [P, 1], F32, early)
        so.spill_row_i = sb("spill_row_i", [P, 1], I32, early)
        so.ones_row = sb("ones_row", [P, COUNT_COLS], F32, early)
        so.spills = sb("spills", [P, COUNT_BUFS, COUNT_COLS], F32, early)
        so.iota_i = sb("bucket_iota_i", [P, NT], I32, early)
        so.iota = sb("bucket_iota", [P, NT], F32, early)
        so.empty = sb("empty_slots", [P, FILL, REC], F32, early)
        so.after = sb("after_bf", [P, P], BF16, early)
        so.ones = sb("ones_bf", [P, P], BF16, early)
        so.onehot = sb("bucket_onehot", [P, 2, COUNT_COLS + 1, NT], BF16, early)
        so.pick = sb("pick", [P, 2, COUNT_COLS, NT], F32, early)
        so.before = sb("before", [P, 2, NT], F32, early)
        so.rank = sb("rank", [P, COUNT_BUFS, COUNT_COLS], F32, early)
        so.place = sb("place", [P, COUNT_BUFS, 4, COUNT_COLS], F32, early)
        so.slot = sb("slot", [P, COUNT_BUFS, COUNT_COLS], I32, early)
        so.rec = sb("rec_out", [P, COUNT_BUFS, COUNT_COLS, REC], F32, early)
        early.close()

        recs = [sb(f"recs{b}", [P, BLOCKS, REC]) for b in range(2)]
        feat = [sb(f"feat{b}", [P, BLOCKS, FEAT]) for b in range(2)]
        onehot = [sb(f"onehot{b}", [P, BLOCKS, TILE_NODES]) for b in range(2)]
        xt = [sb(f"xt{b}", [P, D]) for b in range(2)]
        sums = sb("sums", [P, FEAT])
        sums_t = sb("sums_t", [P, 4 * TILE_NODES])
        vr_t = sb("vr_t", [V, TILE_NODES])
        ys = [sb(f"ys{b}", [P, 2 * S]) for b in range(2)]
        yv = [sb(f"yv{b}", [P, 3, KV]) for b in range(2)]
        yx = [sb(f"yx{b}", [P, 3 * V]) for b in range(2)]
        q3 = sb("q3", [P, 3 * VV])
        ys_t = sb("ys_t", [P, TILE_NODES])
        v_t = sb("v_t", [3 * V, TILE_NODES])
        work = sb("work", [P, 3 * ROUND])
        q = sb("q", [P, V * V])
        q_t = sb("q_t", [P, V * V // P, TILE_NODES])
        upd = sb("upd", [P, D])
        lin = sb("lin", [P, D])
        h = sb("h", [P, D])
        stats = sb("stats", [P, 8])
        sq = sb("sq", [P, D])
        res = [sb(f"res{b}", [P, D]) for b in range(2)]
        spill_in = [sb(f"spill_in{b}", [P, FEAT]) for b in range(2)]
        spill_rows = spill_in[0]
        spill_rec = sb("spill_rec", [P, REC])
        spill_key = sb("spill_key", [P, 8])
        spill_idx = sb("spill_idx", [P, 1], I32)
        spill_same = sb("spill_same", [P, 2, P])

        padded, edges_in, empty_made, emptied = sem("padded"), sem("edges_in"), sem("empty_made"), sem("emptied")
        iotas, consts, keyed, keys_ready = sem("iotas"), sem("consts"), sem("keyed"), sem("keys_ready")
        hot, counted, ranking, ranked, packed = sem("hot"), sem("counted"), sem("ranking"), sem("ranked"), sem("packed")
        scattered = [sem(f"scattered{b}") for b in range(COUNT_BUFS)]
        dma_go = sem("dma_go")
        sort_done, flag_ready, spills_turned = sem("sort_done"), sem("flag_ready"), sem("spills_turned")
        w_zeroed, w_in, w_ready = sem("w_zeroed"), sem("w_in"), sem("w_ready")

        HM = TILE_NODES

        def layer_sems(layer):
            s = {}
            for n in ("hot", "vr_mul", "vr", "scaled", "edges_half", "edges_done", "z_out", "turned", "turned_out", "agg",
                      "y_out", "y_turned", "y_turned_out", "prods", "prods_used", "upd", "q_mul", "q_add",
                      "q_ready", "q_turned", "q_turned_out", "lin", "lin_out", "h_part", "h_ready", "squares",
                      "deviation", "inverse", "normed",
                      "sp_rec", "sp_x", "sp_link", "sp_diag", "sp_keys", "sp_feat", "sp_sum", "sp_idx",
                      "sp_old", "sp_new", "sp_put", "sp_zero", "sp_zeroed", "sp_done"):
                s[n] = sem(f"{n}_l{layer}")
            for n in ("rec_in", "gathered", "x_in", "stored", "spill_in"):
                s[n] = [sem(f"{n}{b}_l{layer}") for b in range(2)]
            return s

        LS = [layer_sems(layer) for layer in range(2)]
        block = whole.enter_context(nc.Block())

        def sweep(eng, step):
            step(0, 0, 0, True, True, False)
            step(1, 0, 1, True, True, True)
            step(2, 1, 0, True, True, True)
            with eng.Fori(1, tiles // 2 - 2) as i:
                step(2 * i + 1, i, 1, True, True, True)
                step(2 * i + 2, i + 1, 0, True, True, True)
            step(tiles - 3, tiles // 2 - 2, 1, True, True, True)
            step(tiles - 2, tiles // 2 - 1, 0, True, True, True)
            step(tiles - 1, tiles // 2 - 1, 1, False, True, True)
            step(tiles, tiles // 2, 0, False, False, True)

        def following(half, b):
            return (half, 1) if b == 0 else (half + 1, 0)

        def before_end(t, n):
            return not isinstance(t, int) or t + n < tiles

        def at_least(t, n):
            return not isinstance(t, int) or t >= n

        @block.sync
        def _(sp):
            sp.wait_ge(padded, 3)
            for to, frm, w in ((so.src_i, src, 1), (so.dst_i, dst, 1), (so.attr, attr, 4)):
                full = (P - 1) * COLS * w
                sp.dma_start(to[0:P - 1, 0:COLS * w], frm[0:full].rearrange("(p c) -> p c", p=P - 1)).then_inc(edges_in, 16)
                sp.dma_start(to[P - 1:P, 0:LAST * w], frm[full:E * w].rearrange("(p c) -> p c", p=1)).then_inc(edges_in, 16)
            sp.wait_ge(empty_made, 2)
            slots_v = slots.rearrange("(p k) c -> p (k c)", p=P)
            for i in range(FILLS):
                sp.dma_start(slots_v[:, i * FILL * REC:(i + 1) * FILL * REC],
                             so.empty[:, :, :].rearrange("p k c -> p (k c)")).then_inc(emptied, 16)
            sp.wait_ge(w_zeroed, 1)
            for layer in range(2):
                w, t = weights[layer], wt[layer]
                mix = t.bil[:, SS:SS + MIX].rearrange("p (w k) -> p w k", k=KV)
                for to, frm in ((t.bil[S:P, 0:SS], w["u_ss"]), (mix[0:S, :, 0:V], w["u_sv"]), (mix[S:P, :, V:KV], w["u_vs"]),
                                (t.vv[:, :, :], w["u_vv"].rearrange("(c p) w -> p c w", p=P)),
                                (t.msg0[0:S, :], w["lm_s"]), (t.msg0[S:P, :], w["m_ss"]),
                                (t.msg1[0:S, :], w["m_sv"]), (t.msg1[S:S + V, :], w["lm_v"]), (t.msg1[S + V:P, :], w["m_vs"]),
                                (t.msg_vr[:, :], w["m_vv"]), (t.lin0[0:S, :], w["lu_s"])):
                    sp.dma_start(to, frm).then_inc(w_in, 16)
                for i in range(3):
                    sp.dma_start(t.lin1[V * i:V * i + V, V * i:V * i + V], w["lu_v"]).then_inc(w_in, 16)
            sp.wait_ge(sort_done, 1)
            sp.wait_ge(flag_ready, 1)
            n_spill = sp.value_load(spill_blocks[0:1, 0:1], min_val=0, max_val=COLS)

            for layer in range(2):
                s = LS[layer]
                table, to = (x, x_mid) if layer == 0 else (x_mid, out)
                if layer == 1:
                    for b in range(2):
                        sp.wait_ge(LS[0]["stored"][b], 16 * (tiles // 2))
                with sp.If(n_spill > 0):
                    sp.wait_ge(s["sp_zero"], 1)
                    zero = feat[0][:, :, :].rearrange("p k c -> p (k c)")
                    rows = spill_sums.rearrange("(p k) c -> p (k c)", p=P)
                    width, piece, n = ZROWS // P * FEAT, BLOCKS * FEAT, 0
                    for a in range(0, width, piece):
                        z = min(piece, width - a)
                        sp.dma_start(rows[:, a:a + z], zero[:, 0:z]).then_inc(s["sp_zeroed"], 16)
                    with sp.Fori(0, n_spill) as k:
                        sp.wait_ge(s["sp_put"], k * 16)
                        sp.dma_start(spill_rec[:, :], slots[bass.ds(k * P + SPILL0, P), :]).then_inc(s["sp_rec"], 16)
                sp.wait_ge(s["sp_done"], 1)

                def load_records(t, b, s=s):
                    sp.dma_start(recs[b][:, :, :], slots[bass.ds(t * CAP, CAP), :].rearrange("(p k) c -> p k c", k=BLOCKS)
                                 ).then_inc(s["rec_in"][b], 16)

                def load_spill_sums(t, b, s=s):
                    with sp.If(n_spill > 0):
                        sp.dma_start(spill_in[b][0:HM, :], spill_sums[bass.ds(t * HM, HM), :]).then_inc(s["spill_in"][b], 16)

                def step(t, half, b, prep, edges, nodes, s=s, table=table, to=to):
                    if before_end(t, 2):
                        sp.wait_ge(s["scaled"], BLOCKS * (t + 1))
                        sp.wait_ge(s["vr"], t + 1)
                        sp.wait_ge(s["hot"], t + 1)
                        load_records(t + 2, b)
                    if edges:
                        if at_least(t, 1):
                            sp.wait_ge(s["edges_done"], t)
                        if at_least(t, 2):
                            sp.wait_ge(s["h_ready"], t - 1)
                            sp.wait_ge(s["q_mul"], t - 1)
                        sp.dma_start(xt[b][0:HM, :], table[bass.ds(t * HM, HM), :]).then_inc(s["x_in"][b], 16)
                    if prep:
                        load_spill_sums(t + 1, 1 - b)
                    if at_least(t, 2):
                        sp.wait_ge(s["normed"], t - 1)
                        sp.dma_start(to[bass.ds((t - 2) * HM, HM), :], res[b][0:HM, :]).then_inc(s["stored"][b], 16)

                load_records(0, 0)
                load_records(1, 1)
                load_spill_sums(0, 0)
                sweep(sp, step)
                sp.wait_ge(s["normed"], tiles)
                sp.dma_start(to[(tiles - 1) * HM:tiles * HM, :], res[1][0:HM, :]).then_inc(s["stored"][1], 16)
            for b in range(2):
                sp.wait_ge(LS[1]["stored"][b], 16 * (tiles // 2))

        @block.gpsimd
        def _(g):
            g.memset(so.src_i[:, :], N).then_inc(padded, 1)
            g.memset(so.dst_i[:, :], 0).then_inc(padded, 1)
            g.memset(so.attr[:, :], 0.0).then_inc(padded, 1)
            g.iota(so.iota_i[:, :], [[1, NT]], base=0, channel_multiplier=0).then_inc(iotas, 1)
            g.iota(so.spill_row_i[:, :], [[0, 1]], base=SPILL0 - P, channel_multiplier=1).then_inc(iotas, 1)
            g.iota(node_iota_i[:, :], [[1, TILE_NODES]], base=0, channel_multiplier=0).then_inc(iotas, 1)
            g.iota(trash_i[:, :], [[0, 1]], base=TRASH, channel_multiplier=1).then_inc(iotas, 1)
            g.memset(ones_f[:, :], 1.0).then_inc(iotas, 1)
            g.memset(so.ones[:, :], 1.0).then_inc(iotas, 1)
            g.wait_ge(iotas, 6)
            g.affine_select(so.after[:, :], so.ones[:, :], [[1, P]], ALU.is_gt, 0.0, base=0, channel_multiplier=-1).then_inc(iotas, 1)
            g.affine_select(after[:, :], ones_f[:, :], [[1, P]], ALU.is_gt, 0.0, base=0, channel_multiplier=-1).then_inc(iotas, 1)
            g.affine_select(ident[:, :], ones_f[:, :], [[1, P]], ALU.is_equal, 0.0, base=0, channel_multiplier=-1).then_inc(iotas, 1)
            last_slot = g.to_reg(SLOTS - 1)
            def carry():
                g.sem_inc(dma_go, 1)

            g.wait_ge(emptied, 16 * FILLS)
            with g.Fori(0, STEPS) as i:
                for b in range(COUNT_BUFS):
                    c = COUNT_BUFS * i + b
                    g.wait_ge(ranked, c + 1)
                    g.wait_ge(packed, 4 * c + 4)
                    carry()
                    for j in range(COUNT_COLS):
                        g.indirect_dma_start(out=slots[:, :], out_offset=bass.IndirectOffsetOnAxis(ap=so.slot[:, b, j:j + 1], axis=0),
                                             in_=so.rec[:, b, j, :], in_offset=None, bounds_check=last_slot, oob_is_err=False
                                             ).then_inc(scattered[b], 16)
            for b in range(COUNT_BUFS):
                g.wait_ge(scattered[b], 16 * COUNT_COLS * STEPS)
            g.nop().then_inc(sort_done, 1)
            g.wait_ge(flag_ready, 1)
            n_spill = g.value_load(spill_blocks[0:1, 0:1], min_val=0, max_val=COLS)

            for layer in range(2):
                s = LS[layer]
                table = x if layer == 0 else x_mid
                if layer == 1:
                    for b in range(2):
                        g.wait_ge(LS[0]["stored"][b], 16 * (tiles // 2))
                with g.If(n_spill > 0):
                    n_zero = -(-(ZROWS // P * FEAT) // (BLOCKS * FEAT))
                    g.wait_ge(s["sp_zeroed"], 16 * n_zero)
                    with g.Fori(0, n_spill) as k:
                        g.wait_ge(s["sp_rec"], 16 * k + 16)
                        carry()
                        g.indirect_dma_start(out=feat[1][:, 0, 0:D], out_offset=None, in_=table[:, :],
                                             in_offset=bass.IndirectOffsetOnAxis(ap=spill_rec[:, 0:1].bitcast(I32), axis=0)
                                             ).then_inc(s["sp_x"], 16)
                        g.wait_ge(s["sp_idx"], k + 1)
                        carry()
                        g.indirect_dma_start(out=spill_rows[:, :], out_offset=None, in_=spill_sums[:, :],
                                             in_offset=bass.IndirectOffsetOnAxis(ap=spill_idx[:, :], axis=0)
                                             ).then_inc(s["sp_old"], 16)
                        g.wait_ge(s["sp_new"], 2 * k + 2)
                        carry()
                        g.indirect_dma_start(out=spill_sums[:, :], out_offset=bass.IndirectOffsetOnAxis(ap=spill_idx[:, :], axis=0),
                                             in_=spill_rows[:, :], in_offset=None).then_inc(s["sp_put"], 16)
                    g.wait_ge(s["sp_put"], 16 * n_spill)
                g.nop().then_inc(s["sp_done"], 1)

                def gather(ks, half, b, *free, s=s, table=table):
                    for f in free:
                        g.wait_ge(*f)
                    g.wait_ge(s["rec_in"][b], 16 * half + 16)
                    carry()
                    for k in ks:
                        g.indirect_dma_start(out=feat[b][:, k, RAW:RAW + D], out_offset=None, in_=table[:, :],
                                             in_offset=bass.IndirectOffsetOnAxis(ap=recs[b][:, k, 0:1].bitcast(I32), axis=0)
                                             ).then_inc(s["gathered"][b], 16)

                def vector_products(n, vrs, nb, nh, s=s):
                    g.wait_ge(s["x_in"][nb], 16 * nh + 16)
                    g.wait_ge(s["y_out"], 4 * n + 4)
                    g.wait_ge(s["q_ready"], n)
                    g.wait_ge(s["vr"], vrs)
                    g.tensor_tensor(q3[0:HM, :].rearrange("p (i u v) -> p i u v", i=3, u=V),
                                    xt[nb][0:HM, S:D].rearrange("p (u i) -> p i u", i=3).unsqueeze(3).broadcast_to([HM, 3, V, V]),
                                    yv[nb][0:HM, :, 0:V].unsqueeze(2).broadcast_to([HM, 3, V, V]), ALU.mult).then_inc(s["q_mul"], 1)
                    g.wait_ge(s["q_mul"], n + 1)
                    g.wait_ge(s["q_turned"], 2 * n)
                    g.tensor_tensor(q[0:HM, :], q3[0:HM, 0:VV], q3[0:HM, VV:2 * VV], ALU.add).then_inc(s["q_add"], 1)
                    g.wait_ge(s["q_add"], n + 1)
                    g.tensor_tensor(q[0:HM, :], q[0:HM, :], q3[0:HM, 2 * VV:3 * VV], ALU.add).then_inc(s["q_ready"], 1)

                def vr_products(t, half, b, after_q, s=s):
                    g.wait_ge(s["gathered"][b], 16 * BLOCKS * half + 16 * BLOCKS)
                    if after_q:
                        g.wait_ge(s["q_ready"], t - 1)
                    elif t > 0:
                        g.wait_ge(s["vr"], t)
                    g.tensor_tensor(q3[:, 0:BLOCKS * 3 * V].rearrange("p (k u i) -> p k u i", u=V, i=3),
                                    feat[b][:, :, S:D].rearrange("p k (u i) -> p k u i", i=3),
                                    recs[b][:, :, 2:5].unsqueeze(2).broadcast_to([P, BLOCKS, V, 3]), ALU.mult).then_inc(s["vr_mul"], 1)

                first, second = range(0, SPLIT), range(SPLIT, BLOCKS)

                def step(t, half, b, prep, edges, nodes, s=s):
                    if prep and at_least(t, 1):
                        gather(second, *following(half, b), (s["edges_done"], t))
                    if nodes:
                        vector_products(t - 1, t + 1 if edges else t, 1 - b, half if b == 1 else half - 1)
                    if prep:
                        vr_products(t + 1, *following(half, b), nodes)
                    if before_end(t, 2):
                        gather(first, half + 1, b, (s["edges_half"], t + 1))

                gather(range(BLOCKS), 0, 0)
                gather(range(BLOCKS), 0, 1)
                vr_products(0, 0, 0, False)
                sweep(g, step)

        @block.vector
        def _(ve):
            ve.memset(so.empty[:, :, :], 0.0).then_inc(empty_made, 1)
            ve.wait_ge(empty_made, 1)
            ve.memset(so.empty[:, :, 1:2], -1.0).then_inc(empty_made, 1)
            for layer in range(2):
                for z in (wt[layer].bil[:, :], wt[layer].lin0[:, :], wt[layer].lin1[:, :]):
                    last = ve.memset(z, 0.0)
            last.then_inc(w_zeroed, 1)
            ve.memset(eps_col[:, :], EPS)
            ve.memset(so.onehot[:, :, :, :], 0.0)
            ve.memset(so.before[:, :, :], 0.0)
            ve.memset(so.spills[:, :, :], 0.0)
            ve.memset(so.ones_row[:, :], 1.0)
            ve.memset(so.rec[:, :, :, :], 0.0).then_inc(consts, 1)
            ve.wait_ge(iotas, 4)
            ve.tensor_copy(so.iota[:, :], so.iota_i[:, :])
            ve.tensor_copy(trash[:, :], trash_i[:, :])
            ve.tensor_copy(node_iota[:, :], node_iota_i[:, :]).then_inc(consts, 1)
            ve.wait_ge(edges_in, 16 * 6)
            n = 0

            def chain(ins):
                nonlocal n
                n += 1
                ins.then_inc(keyed, 1)
                ve.wait_ge(keyed, n)

            bk, lo, tmp = so.bucket[:, :], so.local[:, :], so.tmp[:, :]
            chain(ve.tensor_copy(so.src[:, :], so.src_i[:, :]))
            chain(ve.tensor_scalar(tmp, so.src[:, :], 0.5, 1.0 / TILE_NODES, ALU.add, ALU.mult))
            chain(ve.tensor_scalar(so.bucket_i[:, :], tmp, -0.5, None, ALU.add))
            chain(ve.tensor_copy(bk, so.bucket_i[:, :]))
            chain(ve.scalar_tensor_tensor(lo, bk, -float(TILE_NODES), so.src[:, :], ALU.mult, ALU.add))
            chain(ve.tensor_scalar(tmp, lo, 0.0, None, ALU.is_lt))
            chain(ve.tensor_tensor(bk, bk, tmp, ALU.subtract))
            chain(ve.tensor_scalar(tmp, lo, float(TILE_NODES), None, ALU.is_ge))
            chain(ve.tensor_tensor(bk, bk, tmp, ALU.add))
            chain(ve.scalar_tensor_tensor(lo, bk, -float(TILE_NODES), so.src[:, :], ALU.mult, ALU.add))
            chain(ve.tensor_copy(so.spill_row[:, :], so.spill_row_i[:, :]))
            chain(ve.tensor_scalar(tmp, bk, float(NT), float(1 << 20), ALU.is_ge, ALU.mult))
            chain(ve.scalar_tensor_tensor(so.base[:, :], bk, float(CAP), tmp, ALU.mult, ALU.add))
            ve.nop().then_inc(keys_ready, 1)
            with ve.Fori(0, STEPS) as i:
                for b in range(COUNT_BUFS):
                    c = COUNT_BUFS * i + b
                    o, pb = c * COUNT_COLS, b % 2
                    m = 0
                    hots = so.onehot[:, pb, 0:COUNT_COLS, :]
                    cnt = (sum_lo, sum_hi)[pb][:, 0:(COUNT_COLS + 1) * NT].rearrange("p (j b) -> p j b", b=NT)
                    ve.tensor_tensor(hots, so.bucket[:, bass.ds(o, COUNT_COLS)].unsqueeze(2).broadcast_to([P, COUNT_COLS, NT]),
                                     so.iota[:, :].unsqueeze(1).broadcast_to([P, COUNT_COLS, NT]), ALU.is_equal).then_inc(hot, 1)
                    ve.wait_ge(counted, c + 1)

                    def link(ins):
                        nonlocal m
                        m += 1
                        ins.then_inc(ranking, 1)
                        ve.wait_ge(ranking, 10 * c + m)

                    pick, rank = so.pick[:, pb, :, :], so.rank[:, b, :]
                    pl = [so.place[:, b, k, :] for k in range(4)]
                    link(ve.tensor_tensor(so.before[:, 1 - pb, :], so.before[:, pb, :], cnt[:, COUNT_COLS, :], ALU.add))
                    link(ve.tensor_tensor(pick, cnt[:, 0:COUNT_COLS, :],
                                          so.before[:, pb, :].unsqueeze(1).broadcast_to([P, COUNT_COLS, NT]), ALU.add))
                    link(ve.tensor_tensor(pick, pick, hots, ALU.mult))
                    link(ve.tensor_reduce(rank, pick, AX_X, ALU.add))
                    link(ve.tensor_scalar(pl[0], rank, float(CAP), None, ALU.is_ge))
                    so_far = so.spills[:, b, :]
                    link(ve.tensor_tensor_scan(so_far, so.ones_row[:, :], pl[0], so.spills[:, (b - 1) % COUNT_BUFS, COUNT_COLS - 1:COUNT_COLS], ALU.mult, ALU.add))
                    link(ve.tensor_tensor(pl[1], so.base[:, bass.ds(o, COUNT_COLS)], rank, ALU.add))
                    link(ve.tensor_scalar(pl[2], so_far, float(P), so.spill_row[:, :], ALU.mult, ALU.add))
                    link(ve.tensor_tensor(pl[2], pl[2], pl[1], ALU.subtract))
                    link(ve.tensor_tensor(pl[3], pl[0], pl[2], ALU.mult))
                    ve.wait_ge(scattered[b], 16 * COUNT_COLS * i)
                    ve.tensor_tensor(so.slot[:, b, :], pl[1], pl[3], ALU.add).then_inc(ranked, 1)
            ve.wait_ge(spills_turned, 1)
            ve.tensor_reduce(most[0:1, :], small_ps[0:1, 0:P], AX_X, ALU.max).then_inc(keyed, 1)
            ve.wait_ge(keyed, n + 1)
            ve.tensor_copy(spill_blocks[0:1, :], most[0:1, :]).then_inc(flag_ready, 1)

            ve.wait_ge(w_in, 16 * 14 * 2)
            for layer in range(2):
                k, t = layer_scales(layer), wt[layer]
                mix = t.bil[:, SS:SS + MIX]
                for part, c in ((t.bil[S:P, 0:SS], "u_ss"), (mix[0:S, :], "u_sv"), (mix[S:P, :], "u_vs"),
                                (t.vv[:, :, :], "u_vv"), (t.msg0[0:S, :], "l_s"), (t.msg0[S:P, :], "m_ss"),
                                (t.msg1[0:S, :], "m_sv"), (t.msg1[S:S + V, :], "l_v"), (t.msg1[S + V:P, :], "m_vs"),
                                (t.msg_vr[:, :], "m_vv"), (t.lin0[0:S, :], "l_s"), (t.lin1[:, :], "l_v")):
                    last = ve.tensor_scalar(part, part, float(k[c]), None, ALU.mult)
            last.then_inc(w_ready, 1)
            ve.wait_ge(w_ready, 1)
            ve.wait_ge(flag_ready, 1)
            n_spill = ve.value_load(spill_blocks[0:1, 0:1], min_val=0, max_val=COLS)

            for layer in range(2):
                s = LS[layer]
                SPILL_LINKS = 16
                with ve.If(n_spill > 0):
                    if layer == 1:
                        ve.wait_ge(LS[0]["edges_done"], tiles)
                    else:
                        ve.wait_ge(sort_done, 1)
                    ve.memset(feat[0][:, :, :], 0.0).then_inc(s["sp_zero"], 1)
                    with ve.Fori(0, n_spill) as k:
                        m = 0

                        def link(ins, s=s, k=k):
                            nonlocal m
                            m += 1
                            ins.then_inc(s["sp_link"], 1)
                            ve.wait_ge(s["sp_link"], SPILL_LINKS * k + m)

                        f = feat[1][:, 0, :]
                        key, c8 = spill_rec[:, 6:7], [spill_key[:, j:j + 1] for j in range(8)]
                        ve.wait_ge(s["sp_rec"], 16 * k + 16)
                        link(ve.tensor_scalar(c8[0], spill_rec[:, 1:2], 0.0, None, ALU.is_ge))
                        link(ve.tensor_scalar(c8[1], c8[0], 1.0, None, ALU.subtract))
                        link(ve.scalar_tensor_tensor(c8[2], key, c8[0], c8[1], ALU.mult, ALU.add))
                        ve.tensor_scalar(spill_same[:, 0, :], ident[:, :], c8[2], None, ALU.mult).then_inc(s["sp_diag"], 1)
                        ve.wait_ge(s["sp_keys"], k + 1)
                        link(ve.tensor_scalar(spill_same[:, 1, :], small_ps[:, 0:P], c8[2], None, ALU.is_equal))
                        link(ve.tensor_tensor(spill_same[:, 0, :], spill_same[:, 1, :], after[:, :], ALU.mult))
                        link(ve.tensor_reduce(c8[3], spill_same[:, 0, :], AX_X, ALU.add))
                        link(ve.tensor_scalar(c8[4], c8[3], 0.0, None, ALU.is_equal))
                        link(ve.tensor_tensor(c8[4], c8[4], c8[0], ALU.mult))
                        link(ve.tensor_tensor(c8[5], key, trash[:, :], ALU.subtract))
                        link(ve.tensor_tensor(c8[6], c8[5], c8[4], ALU.mult))
                        ve.tensor_tensor(spill_idx[:, :], c8[6], trash[:, :], ALU.add).then_inc(s["sp_idx"], 1)
                        ve.wait_ge(s["sp_x"], 16 * k + 16)
                        vec = f[:, S:D].rearrange("p (u i) -> p u i", i=3)
                        link(ve.tensor_scalar(f[:, DIST:DIST + D], f[:, 0:D], spill_rec[:, 5:6], None, ALU.mult))
                        link(ve.tensor_scalar(f[:, VR:VR + V], vec[:, :, 0], spill_rec[:, 2:3], None, ALU.mult))
                        link(ve.scalar_tensor_tensor(f[:, VR:VR + V], vec[:, :, 1], spill_rec[:, 3:4], f[:, VR:VR + V], ALU.mult, ALU.add))
                        link(ve.scalar_tensor_tensor(f[:, VR:VR + V], vec[:, :, 2], spill_rec[:, 4:5], f[:, VR:VR + V], ALU.mult, ALU.add))
                        for i in range(3):
                            rs = ve.tensor_scalar(f[:, RS + S * i:RS + S * i + S], f[:, 0:S], spill_rec[:, 2 + i:3 + i], None, ALU.mult)
                            if i < 2:
                                link(rs)
                        rs.then_inc(s["sp_feat"], 1)
                        assert m == SPILL_LINKS
                        ve.wait_ge(s["sp_sum"], k + 1)
                        ve.wait_ge(s["sp_old"], 16 * k + 16)
                        ve.tensor_tensor(spill_rows[:, 0:HALF], spill_rows[:, 0:HALF], sum_lo[:, 0:HALF], ALU.add).then_inc(s["sp_new"], 1)
                        ve.tensor_tensor(spill_rows[:, HALF:FEAT], spill_rows[:, HALF:FEAT], sum_hi[:, 0:FEAT - HALF], ALU.add).then_inc(s["sp_new"], 1)
                ve.wait_ge(s["sp_done"], 1)

                def one_hot(t, half, b, s=s):
                    ve.wait_ge(s["rec_in"][b], 16 * half + 16)
                    if at_least(t, 2):
                        ve.wait_ge(s["edges_done"], t - 1)
                    ve.tensor_tensor(onehot[b][:, :, :], recs[b][:, :, 1:2].broadcast_to([P, BLOCKS, HM]),
                                     node_iota[:, :].unsqueeze(1).broadcast_to([P, BLOCKS, HM]), ALU.is_equal).then_inc(s["hot"], 1)

                def sum_vr(t, b, s=s):
                    ve.wait_ge(s["vr_mul"], t + 1)
                    ve.tensor_reduce(feat[b][:, :, VR:VR + V], q3[:, 0:BLOCKS * 3 * V].rearrange("p (k u i) -> p k u i", u=V, i=3),
                                     AX_X, ALU.add).then_inc(s["vr"], 1)

                def step(t, half, b, prep, edges, nodes, s=s):
                    if prep:
                        one_hot(t + 1, *following(half, b))
                    if not nodes:
                        sum_vr(t + 1, 1 - b)
                        return
                    n, nb, nh = t - 1, 1 - b, (half if b == 1 else half - 1)
                    X = xt[nb][0:HM, :]
                    ve.wait_ge(s["x_in"][nb], 16 * nh + 16)
                    ve.wait_ge(s["upd"], RS_ALL * n)
                    ve.wait_ge(s["h_part"], 3 * n)
                    ve.wait_ge(s["y_out"], 4 * n + 4)
                    for r in range(R0):
                        ve.wait_ge(s["prods"], RS_ALL * n + r + 1)
                        if r >= 2:
                            ve.wait_ge(s["upd"], RS_ALL * n + r - 1)
                        wk = work[0:HM, ROUND * (r % 2):ROUND * (r % 2) + ROUND].rearrange("p (w u) -> p w u", u=S)
                        ve.tensor_tensor(wk, prods_ps[r % 2][0:HM, :].rearrange("p (w u) -> p w u", u=S),
                                         X[:, 0:S].unsqueeze(1).broadcast_to([HM, ROUND // S, S]), ALU.mult).then_inc(s["prods_used"], 1)
                        ve.wait_ge(s["prods_used"], USES * n + used(r))
                        ve.tensor_reduce(upd[0:HM, ROUND // S * r:ROUND // S * (r + 1)], wk, AX_X, ALU.add).then_inc(s["upd"], 1)
                    if at_least(t, 2):
                        normalise(t - 2, half - 1, b, s)
                    if prep:
                        sum_vr(t + 1, 1 - b)
                    wk = work[0:HM, :].rearrange("p (i w k) -> p i w k", i=3, k=KV)
                    upd1 = upd[0:HM, S:D].rearrange("p (w i) -> p i w", i=3)
                    for r in range(R0, R0 + R1):
                        ve.wait_ge(s["prods"], RS_ALL * n + r + 1)
                        ve.wait_ge(s["upd"], RS_ALL * n + r)
                        for i in range(3):
                            ve.tensor_tensor(wk[:, i, :, :], prods_ps[r % 2][0:HM, :].rearrange("p (w k) -> p w k", k=KV),
                                             yv[nb][0:HM, i, :].unsqueeze(1).broadcast_to([HM, ROUND // KV, KV]), ALU.mult).then_inc(s["prods_used"], 1)
                        ve.wait_ge(s["prods_used"], USES * n + used(r))
                        w0 = ROUND // KV * (r - R0)
                        ve.tensor_reduce(upd1[:, :, w0:w0 + ROUND // KV], wk, AX_X, ALU.add).then_inc(s["upd"], 1)
                    ve.wait_ge(s["lin_out"], 2 * n + 2)
                    ve.wait_ge(s["normed"], n)
                    ve.scalar_tensor_tensor(h[0:HM, :], X, 2.0, lin[0:HM, :], ALU.mult, ALU.add).then_inc(s["h_part"], 1)
                    ve.wait_ge(s["upd"], RS_ALL * n + RS_ALL)
                    ve.wait_ge(s["h_part"], 3 * n + 1)
                    ve.tensor_tensor(h[0:HM, :], h[0:HM, :], upd[0:HM, :], ALU.add).then_inc(s["h_part"], 1)
                    ve.wait_ge(s["h_part"], 3 * n + 2)
                    ve.tensor_reduce(stats[0:HM, 0:1], h[0:HM, :], AX_X, ALU.add).then_inc(s["h_part"], 1)
                    ve.wait_ge(s["h_part"], 3 * n + 3)
                    ve.tensor_scalar(stats[0:HM, 1:2], stats[0:HM, 0:1], -1.0 / D, None, ALU.mult).then_inc(s["h_ready"], 1)

                def normalise(n, half, b, s):
                    ve.wait_ge(s["deviation"], n + 1)
                    ve.wait_ge(s["stored"][b], 16 * half)
                    ve.reciprocal(stats[0:HM, 4:5], stats[0:HM, 3:4]).then_inc(s["inverse"], 1)
                    ve.wait_ge(s["inverse"], n + 1)
                    ve.tensor_scalar(res[b][0:HM, :], h[0:HM, :], stats[0:HM, 1:2], stats[0:HM, 4:5], ALU.add, ALU.mult
                                     ).then_inc(s["normed"], 1)

                one_hot(0, 0, 0)
                sum_vr(0, 0)
                sweep(ve, step)
                normalise(tiles - 1, tiles // 2 - 1, 1, s)

        @block.tensor
        def _(te):
            te.wait_ge(iotas, 9)
            te.wait_ge(consts, 1)
            with te.Fori(0, STEPS) as i:
                for b in range(COUNT_BUFS):
                    te.wait_ge(hot, COUNT_BUFS * i + b + 1)
                    cnt = (sum_lo, sum_hi)[b % 2][:, 0:(COUNT_COLS + 1) * NT]
                    hots = so.onehot[:, b % 2, :, :].rearrange("p j b -> p (j b)")
                    te.matmul(cnt, so.after[:, :], hots, start=True, stop=False)
                    for c in range(1, COUNT_COLS + 1):
                        mm = te.matmul(cnt[:, c * NT:], so.ones[:, :], hots[:, 0:(COUNT_COLS + 1 - c) * NT],
                                       start=False, stop=(c == COUNT_COLS))
                    mm.then_inc(counted, 1)
            te.wait_ge(ranked, COUNT_BUFS * STEPS)
            te.transpose(small_ps[0:1, 0:P], so.spills[:, COUNT_BUFS - 1, COUNT_COLS - 1:COUNT_COLS], ident[:, :]).then_inc(spills_turned, 1)
            te.wait_ge(w_ready, 1)
            te.wait_ge(flag_ready, 1)
            n_spill = te.value_load(spill_blocks[0:1, 0:1], min_val=0, max_val=COLS)
            for layer in range(2):
                s, w = LS[layer], wt[layer]
                with te.If(n_spill > 0):
                    with te.Fori(0, n_spill) as k:
                        te.wait_ge(s["sp_diag"], k + 1)
                        te.matmul(small_ps[:, 0:P], ones_f[:, :], spill_same[:, 0, :], start=True, stop=True).then_inc(s["sp_keys"], 1)
                        te.wait_ge(s["sp_feat"], k + 1)
                        te.matmul(sum_lo[:, 0:HALF], spill_same[:, 1, :], feat[1][:, 0, 0:HALF], start=True, stop=True)
                        te.matmul(sum_hi[:, 0:FEAT - HALF], spill_same[:, 1, :], feat[1][:, 0, HALF:FEAT],
                                  start=True, stop=True).then_inc(s["sp_sum"], 1)
                te.wait_ge(s["sp_done"], 1)

                def sum_edges(t, half, b, ks, s=s):
                    for k in ks:
                        if k == 0:
                            te.wait_ge(s["hot"], t + 1)
                            te.wait_ge(s["vr"], t + 1)
                        te.wait_ge(s["scaled"], BLOCKS * t + k + 1)
                        lhs = onehot[b][:, k, :]
                        te.matmul(sum_lo[0:HM, 0:HALF], lhs, feat[b][:, k, 0:HALF], start=(k == 0), stop=(k == BLOCKS - 1))
                        mm = te.matmul(sum_hi[0:HM, 0:FEAT - HALF], lhs, feat[b][:, k, HALF:FEAT], start=(k == 0), stop=(k == BLOCKS - 1))
                        if k == 0:
                            with te.If(n_spill > 0):
                                te.wait_ge(s["spill_in"][b], 16 * half + 16)
                                te.matmul(sum_lo[0:HM, 0:HALF], ident[0:HM, 0:HM], spill_in[b][0:HM, 0:HALF], start=False, stop=False)
                                te.matmul(sum_hi[0:HM, 0:FEAT - HALF], ident[0:HM, 0:HM], spill_in[b][0:HM, HALF:FEAT], start=False, stop=False)
                        if k == SPLIT - 1:
                            mm.then_inc(s["edges_half"], 1)
                        if k == BLOCKS - 1:
                            mm.then_inc(s["edges_done"], 1)

                def step(t, half, b, prep, edges, nodes, s=s, w=w):
                    def some_edges(k0, k1):
                        if edges:
                            sum_edges(t, half, b, range(k0, k1))

                    if not nodes:
                        some_edges(0, BLOCKS)
                        return
                    n = t - 1
                    nb = 1 - b
                    idn = ident[0:HM, 0:HM]

                    def turn_q(part):
                        for c in range(QC // 2):
                            mm = te.transpose(turn_ps[:, HM * c:HM * c + HM], q[0:HM, P * (c + part * QC // 2):P * (c + part * QC // 2 + 1)], idn)
                        mm.then_inc(s["q_turned"], 1)

                    def bilinear(r):
                        if r >= 2:
                            te.wait_ge(s["prods_used"], USES * n + used(r - 2))
                        elif at_least(n, 1) and at_least(t, 2):
                            te.wait_ge(s["prods_used"], USES * n - USES + used(r + RS_ALL - 2))
                        for hh in range(2):
                            c = ROUND * r + 512 * hh
                            rows = slice(S, P) if c < SS else slice(0, P)
                            mm = te.matmul(prods_ps[r % 2][0:HM, 512 * hh:512 * hh + 512], ys_t[rows, :], w.bil[rows, c:c + 512],
                                           start=True, stop=True)
                        mm.then_inc(s["prods"], 1)

                    te.wait_ge(s["z_out"], 4 * n + 4)
                    te.wait_ge(s["q_turned_out"], 2 * n)
                    for c in range(4):
                        te.transpose(turn_ps[:, HM * c:HM * c + HM], sums[0:HM, P * c:P * c + P], idn)
                    te.wait_ge(s["lin_out"], 2 * n)
                    te.transpose(small_ps[0:V, VRT], sums[0:HM, 4 * P:FEAT], idn).then_inc(s["turned"], 1)
                    some_edges(0, 2)
                    te.wait_ge(s["turned_out"], 2 * n + 2)
                    te.matmul(small_ps[0:HM, D:D + S], sums_t[:, 0:HM], w.msg0[:, :], start=True, stop=False)
                    te.matmul(small_ps[0:HM, D:D + S], vr_t[:, :], w.msg_vr[:, :], start=False, stop=True)
                    for i in range(3):
                        mm = te.matmul(small_ps[0:HM, D + S + V * i:D + S + V * i + V], sums_t[:, HM * (i + 1):HM * (i + 2)], w.msg1[:, :],
                                       start=True, stop=True)
                    mm.then_inc(s["agg"], 1)
                    some_edges(2, 3)
                    te.wait_ge(s["y_out"], 4 * n + 4)
                    te.transpose(turn_ps[:, 0:HM], ys[nb][0:HM, :], idn)
                    te.transpose(turn_ps[0:3 * V, HM:2 * HM], yx[nb][0:HM, :], idn).then_inc(s["y_turned"], 1)
                    some_edges(3, 4)
                    te.wait_ge(s["y_turned_out"], 2 * n + 2)
                    bilinear(0)
                    bilinear(1)
                    some_edges(4, 5)
                    bilinear(2)
                    some_edges(5, 7)
                    bilinear(3)
                    some_edges(7, 10)
                    te.wait_ge(s["q_ready"], n + 1)
                    turn_q(0)
                    bilinear(4)
                    some_edges(10, 12)
                    te.wait_ge(s["q_turned_out"], 2 * n + 1)
                    turn_q(1)
                    some_edges(12, BLOCKS)
                    bilinear(5)
                    te.wait_ge(s["q_turned_out"], 2 * n + 2)
                    te.matmul(small_ps[0:HM, S:D], v_t[:, :], w.lin1[:, :], start=True, stop=True)
                    te.matmul(small_ps[0:HM, 0:S], ys_t[:, :], w.lin0[:, :], start=True, stop=False)
                    for c in range(QC):
                        mm = te.matmul(small_ps[0:HM, 0:S], q_t[:, c, :], w.vv[:, c, :], start=False, stop=(c == QC - 1))
                    mm.then_inc(s["lin"], 1)

                sweep(te, step)

        @block.scalar
        def _(ac):
            ac.wait_ge(keys_ready, 1)
            with ac.Fori(0, STEPS) as i:
                for b in range(COUNT_BUFS):
                    o = (COUNT_BUFS * i + b) * COUNT_COLS
                    cols = bass.ds(o, COUNT_COLS)
                    ac.wait_ge(scattered[b], 16 * COUNT_COLS * i)
                    ac.copy(so.rec[:, b, :, 0:1].bitcast(I32), so.dst_i[:, cols].unsqueeze(2)).then_inc(packed, 1)
                    ac.copy(so.rec[:, b, :, 1:2], so.local[:, cols].unsqueeze(2)).then_inc(packed, 1)
                    ac.copy(so.rec[:, b, :, 2:6], so.attr[:, bass.ds(o * 4, COUNT_COLS * 4)].rearrange("p (j f) -> p j f", f=4)
                            ).then_inc(packed, 1)
                    ac.copy(so.rec[:, b, :, 6:7], so.src[:, cols].unsqueeze(2)).then_inc(packed, 1)
            for layer in range(2):
                s = LS[layer]

                def deviation(n, s=s):
                    ac.wait_ge(s["h_ready"], n + 1)
                    ac.activation(sq[0:HM, :], h[0:HM, :], ACT.Square, bias=stats[0:HM, 1:2], accum_out=stats[0:HM, 2:3]).then_inc(s["squares"], 1)
                    ac.wait_ge(s["squares"], n + 1)
                    ac.activation(stats[0:HM, 3:4], stats[0:HM, 2:3], ACT.Sqrt, bias=eps_col[0:HM, :], scale=1.0 / D).then_inc(s["deviation"], 1)

                def scale_edges(t, half, b, ks, s=s):
                    for k in ks:
                        if k == 0:
                            ac.wait_ge(s["gathered"][b], 16 * BLOCKS * half + 16 * BLOCKS)
                        f = feat[b][:, k, :]
                        ac.activation(f[:, DIST:DIST + D], f[:, RAW:RAW + D], ACT.Copy, scale=recs[b][:, k, 5:6])
                        for i in range(3):
                            last = ac.activation(f[:, RS + S * i:RS + S * i + S], f[:, RAW:RAW + S], ACT.Copy, scale=recs[b][:, k, 2 + i:3 + i])
                        last.then_inc(s["scaled"], 1)

                def linear_part(n, s=s):
                    ac.wait_ge(s["lin"], n + 1)
                    ac.wait_ge(s["h_part"], 3 * n)
                    ac.copy(lin[0:HM, 0:S], small_ps[0:HM, 0:S]).then_inc(s["lin_out"], 1)
                    ac.copy(lin[0:HM, S:D].rearrange("p (u i) -> p u i", i=3),
                            small_ps[0:HM, S:D].rearrange("p (i u) -> p u i", i=3)).then_inc(s["lin_out"], 1)

                def step(t, half, b, prep, edges, nodes, s=s):
                    def scale_next(k0, k1):
                        if prep:
                            scale_edges(t + 1, *following(half, b), range(k0, k1))

                    if not nodes:
                        scale_next(0, BLOCKS)
                        return
                    n, nb, nh = t - 1, 1 - b, (half if b == 1 else half - 1)
                    ac.wait_ge(s["x_in"][nb], 16 * nh + 16)
                    if at_least(t, 3):
                        ac.wait_ge(s["y_turned"], n - 1)
                        ac.wait_ge(s["prods_used"], USES * (n - 1))
                        ac.wait_ge(s["q_mul"], n - 1)
                    xv = xt[nb][0:HM, S:D].rearrange("p (u i) -> p i u", i=3)
                    ac.copy(ys[nb][0:HM, 0:S], xt[nb][0:HM, 0:S]).then_inc(s["y_out"], 1)
                    ac.copy(yx[nb][0:HM, :].rearrange("p (i u) -> p i u", i=3), xv)
                    ac.copy(yv[nb][0:HM, :, V:KV], xv).then_inc(s["y_out"], 1)
                    ac.wait_ge(s["edges_done"], n + 1)
                    lo = sum_lo[0:HM, 0:HALF].rearrange("p (c f) -> p c f", c=2)
                    groups = sums[0:HM, P:4 * P].rearrange("p (i f) -> p i f", i=3)
                    ac.copy(sums[0:HM, 0:P].rearrange("p (c f) -> p c f", c=2), lo[:, :, 0:S]).then_inc(s["z_out"], 1)
                    ac.copy(groups[:, :, S:P].rearrange("p i (c u) -> p i c u", c=2),
                            lo[:, :, S:D].rearrange("p c (u i) -> p i c u", i=3)).then_inc(s["z_out"], 1)
                    ac.copy(groups[:, :, 0:S], sum_hi[0:HM, V:V + 3 * S].rearrange("p (i f) -> p i f", i=3)).then_inc(s["z_out"], 1)
                    ac.copy(sums[0:HM, 4 * P:FEAT], sum_hi[0:HM, 0:V]).then_inc(s["z_out"], 1)
                    if at_least(t, 2):
                        linear_part(t - 2)
                    ac.wait_ge(s["turned"], n + 1)
                    ac.copy(sums_t[:, :], turn_ps[:, 0:4 * HM]).then_inc(s["turned_out"], 1)
                    ac.copy(vr_t[:, :], small_ps[0:V, VRT]).then_inc(s["turned_out"], 1)
                    ac.wait_ge(s["agg"], n + 1)
                    ac.copy(ys[nb][0:HM, S:2 * S], small_ps[0:HM, D:D + S]).then_inc(s["y_out"], 1)
                    ac.copy(yv[nb][0:HM, :, 0:V], small_ps[0:HM, D + S:2 * D].rearrange("p (i u) -> p i u", i=3)).then_inc(s["y_out"], 1)
                    ac.wait_ge(s["y_turned"], n + 1)
                    ac.copy(ys_t[:, :], turn_ps[:, 0:HM]).then_inc(s["y_turned_out"], 1)
                    ac.copy(v_t[:, :], turn_ps[0:3 * V, HM:2 * HM]).then_inc(s["y_turned_out"], 1)
                    if at_least(t, 2):
                        deviation(t - 2)
                    for part, (k0, k1) in enumerate(((0, 8), (8, 10))):
                        scale_next(k0, k1)
                        ac.wait_ge(s["q_turned"], 2 * n + part + 1)
                        ac.copy(q_t[:, QC // 2 * part:QC // 2 * (part + 1), :], turn_ps[:, 0:QC // 2 * HM].rearrange("p (c n) -> p c n", n=HM)
                                ).then_inc(s["q_turned_out"], 1)
                    scale_next(10, BLOCKS)

                scale_edges(0, 0, 0, range(0, BLOCKS))
                sweep(ac, step)
                linear_part(tiles - 1)
                deviation(tiles - 1)


_WEIGHTS = {
    "m_ss": ("L0_gnn_wm000", "L1_gnn_Wm_ss"), "m_vv": ("L0_gnn_wm110", "L1_gnn_Wm_vv"),
    "m_sv": ("L0_gnn_wm011", "L1_gnn_Wm_sv"), "m_vs": ("L0_gnn_wm101", "L1_gnn_Wm_vs"),
    "lm_s": ("L0_gnn_lm0", "L1_gnn_Lm_s"), "lm_v": ("L0_gnn_lm1", "L1_gnn_Lm_v"),
    "lu_s": ("L0_gnn_lu0", "L1_gnn_Lu_s"), "lu_v": ("L0_gnn_lu1", "L1_gnn_Lu_v"),
    "u_ss": ("L0_gnn_wu000", "L1_gnn_Wu_ss"), "u_sv": ("L0_gnn_wu011", "L1_gnn_Wu_sv"),
    "u_vs": ("L0_gnn_wu101", "L1_gnn_Wu_vs"), "u_vv": ("L0_gnn_wu110", "L1_gnn_Wu_vv"),
}


def laid_out(name, a):
    if name in ("u_ss", "u_vs"):
        a = a.transpose(1, 2, 0)
        return np.ascontiguousarray(a.reshape(S, SS) if name == "u_ss" else a)
    if name == "u_sv":
        return np.ascontiguousarray(a.transpose(0, 2, 1))
    if name == "u_vv":
        return np.ascontiguousarray(a.reshape(V * V, S))
    return np.ascontiguousarray(a.reshape(-1, a.shape[-1]))


def kernel(**inputs):
    import concourse.bacc as bacc
    from concourse.bass_utils import run_bass_kernel_spmd

    nc = bacc.Bacc("TRN2", target_bir_lowering=False, num_devices=1)
    arrays = {}

    def given(name, a):
        arrays[name] = a
        return nc.dram_tensor(name, a.shape, mybir.dt.from_np(a.dtype), kind="ExternalInput").ap()

    x = given("x", np.ascontiguousarray(inputs["x"]))
    src = given("src", np.ascontiguousarray(inputs["src"]))
    dst = given("dst", np.ascontiguousarray(inputs["dst"]))
    attr = given("edge_attr", np.ascontiguousarray(inputs["edge_attr_4"]).reshape(-1))
    weights = [{k: given(f"{k}_{layer}", laid_out(k, np.asarray(inputs[names[layer]])))
                for k, names in _WEIGHTS.items()} for layer in range(2)]
    out = nc.dram_tensor("out", inputs["x"].shape, F32, kind="ExternalOutput").ap()
    build(nc, x, src, dst, attr, weights, out)
    r = run_bass_kernel_spmd(nc, [arrays], core_ids=[0])
    return r.results[0]["out"]
```

```python
from contextlib import ExitStack

import concourse.bass as bass
import numpy as np
from concourse import mybir

ALU = mybir.AluOpType
ACT = mybir.ActivationFunctionType
AX_X = mybir.AxisListType.X
F32 = mybir.dt.float32
I32 = mybir.dt.int32
BF16 = mybir.dt.bfloat16

P = 128
S = 64
V = 32
D = S + 3 * V
TILE_NODES = 125
BLOCKS = 17
CAP = BLOCKS * P
REC = 8
SPLIT = 9
COUNT_COLS = 4
COUNT_BUFS = 4
EPS = 1e-5

RAW, DIST, VR, RS = 0, D, 2 * D, 2 * D + V
FEAT = RS + 3 * S
HALF = 2 * D

SS = S * S
KV = 2 * V
MIX = V * KV
VV = V * V
QC = VV // P
ROUND = 1024
R0, R1 = SS // ROUND, MIX // ROUND
RS_ALL = R0 + R1
USES = R0 + 3 * R1


def used(r):
    return r + 1 if r < R0 else R0 + 3 * (r + 1 - R0)


class Named:
    pass


def layer_scales(layer):
    i3 = 1.0 / np.sqrt(3.0)
    if layer == 0:
        m, f0, f1 = 1.0 / np.sqrt(S + V), 1.0 / np.sqrt(S * S + V * V), 1.0 / np.sqrt(2 * S * V)
        return dict(m_ss=m, m_vv=i3 * m, m_sv=m, m_vs=m, l_s=S ** -0.5, l_v=V ** -0.5,
                    u_ss=f0, u_vv=i3 * f0, u_sv=f1, u_vs=f1)
    return dict(m_ss=S ** -0.5, m_vv=i3 * V ** -0.5, m_sv=S ** -0.5, m_vs=V ** -0.5,
                l_s=S ** -0.5, l_v=V ** -0.5, u_ss=1.0 / S, u_vv=i3 / V,
                u_sv=(S * V) ** -0.5, u_vs=(S * V) ** -0.5)


def build(nc, x, src, dst, attr, weights, out, tiles=None):
    N = x.shape[0]
    E = src.shape[0]
    NT = N // TILE_NODES
    assert NT * TILE_NODES == N and NT % 2 == 0
    COLS = -(-E // P)
    LAST = E - (P - 1) * COLS
    GROUP = COUNT_COLS * COUNT_BUFS
    STEPS = -(-COLS // GROUP)
    W = STEPS * GROUP
    SPILL0 = NT * CAP
    SLOTS = SPILL0 + COLS * P
    FILL = next(k for k in range(256, 0, -1) if SLOTS // P % k == 0)
    FILLS = SLOTS // P // FILL
    assert FILLS * FILL * P == SLOTS and 0 < LAST <= COLS and (COUNT_COLS + 1) * NT <= 512
    TRASH = N
    tiles = tiles or NT

    slots = nc.dram_tensor("slots", [SLOTS, REC], F32).ap()
    x_mid = nc.dram_tensor("x_mid", [N, D], F32).ap()
    ZROWS = -(-(N + P) // P) * P
    spill_sums_of = [nc.dram_tensor(f"spill_sums{layer}", [ZROWS, FEAT], F32).ap() for layer in range(2)]
    ZERO = next(k for k in range(16, 0, -1) if ZROWS // P % k == 0)
    ZEROS = ZROWS // P // ZERO

    with ExitStack() as whole:
        def sb(name, shape, dt=F32, ctx=whole):
            return ctx.enter_context(nc.sbuf_tensor(name, shape, dt))

        def sem(name):
            return whole.enter_context(nc.semaphore(name))

        def bank(name, n=1):
            return whole.enter_context(nc.psum_tensor(name, [P, 512 * n], F32))

        sum_lo, sum_hi = bank("sum_lo"), bank("sum_hi")
        prods_ps = [bank("prods_ps0", 2), bank("prods_ps1", 2)]
        turn_ps = bank("turn_ps")
        small_ps = bank("small_ps")
        VRT = slice(2 * D, 2 * D + TILE_NODES)

        ident = sb("ident", [P, P])
        after = sb("after", [P, P])
        ones_f = sb("ones_f", [P, P])
        node_iota_i = sb("node_iota_i", [P, TILE_NODES], I32)
        node_iota = sb("node_iota", [P, TILE_NODES])
        eps_col = sb("eps_col", [P, 1])
        spill_blocks = sb("spill_blocks", [P, 1], I32)
        most = sb("most", [P, 1])
        trash_i = sb("trash_i", [P, 1], I32)
        trash = sb("trash", [P, 1])
        wt = []
        for layer in range(2):
            t = Named()
            t.bil = sb(f"w_bil{layer}", [P, SS + MIX])
            t.vv = sb(f"w_vv{layer}", [P, QC, S])
            t.msg0 = sb(f"w_msg0{layer}", [P, S])
            t.msg1 = sb(f"w_msg1{layer}", [P, V])
            t.msg_vr = sb(f"w_msg_vr{layer}", [V, S])
            t.lin0 = sb(f"w_lin0{layer}", [P, S])
            t.lin1 = sb(f"w_lin1{layer}", [3 * V, 3 * V])
            wt.append(t)

        early = ExitStack()
        so = Named()
        so.src_i = sb("src_i", [P, W], I32, early)
        so.dst_i = sb("dst_i", [P, W], I32, early)
        so.attr = sb("attr_sb", [P, W * 4], F32, early)
        so.src = sb("src_f", [P, W], F32, early)
        so.bucket_i = sb("bucket_i", [P, W], I32, early)
        so.bucket = sb("bucket", [P, W], F32, early)
        so.local = sb("local", [P, W], F32, early)
        so.tmp = sb("sort_tmp", [P, W], F32, early)
        so.base = sb("slot_base", [P, W], F32, early)
        so.spill_row = sb("spill_row", [P, 1], F32, early)
        so.spill_row_i = sb("spill_row_i", [P, 1], I32, early)
        so.ones_row = sb("ones_row", [P, 2 * COUNT_COLS], F32, early)
        so.spills = sb("spills", [P, COUNT_BUFS, COUNT_COLS], F32, early)
        so.iota_i = sb("bucket_iota_i", [P, NT], I32, early)
        so.iota = sb("bucket_iota", [P, NT], F32, early)
        so.empty = sb("empty_slots", [P, FILL, REC], F32, early)
        so.zero = sb("zero_rows", [P, ZERO * FEAT], F32, early)
        so.after = sb("after_bf", [P, P], BF16, early)
        so.ones = sb("ones_bf", [P, P], BF16, early)
        so.onehot = sb("bucket_onehot", [P, 2, COUNT_COLS + 1, NT], BF16, early)
        so.pick = sb("pick", [P, 2, COUNT_COLS, NT], F32, early)
        so.before = sb("before", [P, 2, NT], F32, early)
        so.rank = sb("rank", [P, COUNT_BUFS, COUNT_COLS], F32, early)
        so.place = sb("place", [P, COUNT_BUFS // 2, 4, 2 * COUNT_COLS], F32, early)
        so.slot = sb("slot", [P, COUNT_BUFS, COUNT_COLS], I32, early)
        so.rec = sb("rec_out", [P, COUNT_BUFS, COUNT_COLS, REC], F32, early)
        early.close()

        recs = [sb(f"recs{b}", [P, BLOCKS, REC]) for b in range(2)]
        feat = [sb(f"feat{b}", [P, BLOCKS, FEAT]) for b in range(2)]
        onehot = [sb(f"onehot{b}", [P, BLOCKS, TILE_NODES]) for b in range(2)]
        xt = [sb(f"xt{b}", [P, D]) for b in range(2)]
        sums = sb("sums", [P, FEAT])
        sums_t = sb("sums_t", [P, 4 * TILE_NODES])
        vr_t = sb("vr_t", [V, TILE_NODES])
        ys = [sb(f"ys{b}", [P, 2 * S]) for b in range(2)]
        yv = [sb(f"yv{b}", [P, 3, KV]) for b in range(2)]
        yx = [sb(f"yx{b}", [P, 3 * V]) for b in range(2)]
        q3 = sb("q3", [P, 3 * VV])
        ys_t = sb("ys_t", [P, TILE_NODES])
        v_t = sb("v_t", [3 * V, TILE_NODES])
        work = sb("work", [P, 3 * ROUND])
        q = sb("q", [P, V * V])
        q_t = sb("q_t", [P, V * V // P, TILE_NODES])
        upd = sb("upd", [P, D])
        lin = sb("lin", [P, D])
        h = sb("h", [P, D])
        stats = sb("stats", [P, 8])
        sq = sb("sq", [P, D])
        res = [sb(f"res{b}", [P, D]) for b in range(2)]
        spill_in = [sb(f"spill_in{b}", [P, FEAT]) for b in range(2)]
        spill_rows = spill_in[0]
        spill_rec = sb("spill_rec", [P, REC])
        spill_key = sb("spill_key", [P, 8])
        spill_idx = sb("spill_idx", [P, 1], I32)
        spill_same = sb("spill_same", [P, 2, P])

        padded, src_in, edges_in, empty_made, emptied = sem("padded"), sem("src_in"), sem("edges_in"), sem("empty_made"), sem("emptied")
        iotas, consts, keyed, keys_ready = sem("iotas"), sem("consts"), sem("keyed"), sem("keys_ready")
        hot, counted, ranking, ranked, packed = sem("hot"), sem("counted"), sem("ranking"), sem("ranked"), sem("packed")
        scattered = [sem(f"scattered{b}") for b in range(COUNT_BUFS)]
        dma_go = sem("dma_go")
        zero_made, zeroed = sem("zero_made"), sem("zeroed")
        sort_done, flag_ready, spills_turned = sem("sort_done"), sem("flag_ready"), sem("spills_turned")
        w_zeroed, w_in, w_ready = sem("w_zeroed"), sem("w_in"), sem("w_ready")

        HM = TILE_NODES

        def layer_sems(layer):
            s = {}
            for n in ("hot", "vr_mul", "vr", "scaled", "edges_half", "edges_done", "z_out", "z_full", "turned", "turned_out", "agg",
                      "y_out", "y_turned", "y_turned_out", "prods", "prods_used", "upd", "q_mul", "q_add",
                      "q_ready", "q_turned", "q_turned_out", "lin", "lin_out", "h_part", "h_ready", "squares",
                      "deviation", "inverse", "normed",
                      "sp_rec", "sp_x", "sp_link", "sp_diag", "sp_keys", "sp_feat", "sp_sum", "sp_idx",
                      "sp_old", "sp_new", "sp_put", "sp_done"):
                s[n] = sem(f"{n}_l{layer}")
            for n in ("rec_in", "gathered", "x_in", "stored", "spill_in"):
                s[n] = [sem(f"{n}{b}_l{layer}") for b in range(2)]
            return s

        LS = [layer_sems(layer) for layer in range(2)]
        block = whole.enter_context(nc.Block())

        def sweep(eng, step):
            step(0, 0, 0, True, True, False)
            step(1, 0, 1, True, True, True)
            step(2, 1, 0, True, True, True)
            with eng.Fori(1, tiles // 2 - 2) as i:
                step(2 * i + 1, i, 1, True, True, True)
                step(2 * i + 2, i + 1, 0, True, True, True)
            step(tiles - 3, tiles // 2 - 2, 1, True, True, True)
            step(tiles - 2, tiles // 2 - 1, 0, True, True, True)
            step(tiles - 1, tiles // 2 - 1, 1, False, True, True)
            step(tiles, tiles // 2, 0, False, False, True)

        def following(half, b):
            return (half, 1) if b == 0 else (half + 1, 0)

        def before_end(t, n):
            return not isinstance(t, int) or t + n < tiles

        def at_least(t, n):
            return not isinstance(t, int) or t >= n

        @block.sync
        def _(sp):
            def load_edges(to, frm, w, loaded):
                full = (P - 1) * COLS * w
                sp.dma_start(to[0:P - 1, 0:COLS * w], frm[0:full].rearrange("(p c) -> p c", p=P - 1)).then_inc(loaded, 16)
                sp.dma_start(to[P - 1:P, 0:LAST * w], frm[full:E * w].rearrange("(p c) -> p c", p=1)).then_inc(loaded, 16)

            sp.wait_ge(padded, 1)
            load_edges(so.src_i, src, 1, src_in)
            sp.wait_ge(empty_made, 2)
            slots_v = slots.rearrange("(p k) c -> p (k c)", p=P)
            for i in range(FILLS):
                sp.dma_start(slots_v[:, i * FILL * REC:(i + 1) * FILL * REC],
                             so.empty[:, :, :].rearrange("p k c -> p (k c)")).then_inc(emptied, 16)
            sp.wait_ge(padded, 3)
            load_edges(so.dst_i, dst, 1, edges_in)
            load_edges(so.attr, attr, 4, edges_in)
            sp.wait_ge(w_zeroed, 1)
            for layer in range(2):
                w, t = weights[layer], wt[layer]
                mix = t.bil[:, SS:SS + MIX].rearrange("p (w k) -> p w k", k=KV)
                for to, frm in ((t.bil[S:P, 0:SS], w["u_ss"]), (mix[0:S, :, 0:V], w["u_sv"]), (mix[S:P, :, V:KV], w["u_vs"]),
                                (t.vv[:, :, :], w["u_vv"].rearrange("(c p) w -> p c w", p=P)),
                                (t.msg0[0:S, :], w["lm_s"]), (t.msg0[S:P, :], w["m_ss"]),
                                (t.msg1[0:S, :], w["m_sv"]), (t.msg1[S:S + V, :], w["lm_v"]), (t.msg1[S + V:P, :], w["m_vs"]),
                                (t.msg_vr[:, :], w["m_vv"]), (t.lin0[0:S, :], w["lu_s"])):
                    sp.dma_start(to, frm).then_inc(w_in, 16)
                for i in range(3):
                    sp.dma_start(t.lin1[V * i:V * i + V, V * i:V * i + V], w["lu_v"]).then_inc(w_in, 16)
            sp.wait_ge(zero_made, 1)
            pace = COUNT_BUFS * STEPS // (2 * ZEROS)
            for layer, sums_dram in enumerate(spill_sums_of):
                rows = sums_dram.rearrange("(p k) c -> p (k c)", p=P)
                for i in range(ZEROS):
                    sp.wait_ge(ranked, pace * (ZEROS * layer + i))
                    sp.dma_start(rows[:, i * ZERO * FEAT:(i + 1) * ZERO * FEAT], so.zero[:, :]).then_inc(zeroed, 16)
            sp.wait_ge(sort_done, 1)
            sp.wait_ge(flag_ready, 1)
            n_spill = sp.value_load(spill_blocks[0:1, 0:1], min_val=0, max_val=COLS)

            for layer in range(2):
                s = LS[layer]
                table, to = (x, x_mid) if layer == 0 else (x_mid, out)
                if layer == 1:
                    for b in range(2):
                        sp.wait_ge(LS[0]["stored"][b], 16 * (tiles // 2))
                with sp.If(n_spill > 0):
                    with sp.Fori(0, n_spill) as k:
                        sp.wait_ge(s["sp_put"], k * 16)
                        sp.dma_start(spill_rec[:, :], slots[bass.ds(k * P + SPILL0, P), :]).then_inc(s["sp_rec"], 16)
                sp.wait_ge(s["sp_done"], 1)

                def load_records(t, b, s=s):
                    sp.dma_start(recs[b][:, :, :], slots[bass.ds(t * CAP, CAP), :].rearrange("(p k) c -> p k c", k=BLOCKS)
                                 ).then_inc(s["rec_in"][b], 16)

                def load_spill_sums(t, b, s=s, spill_sums=spill_sums_of[layer]):
                    sp.dma_start(spill_in[b][0:HM, :], spill_sums[bass.ds(t * HM, HM), :]).then_inc(s["spill_in"][b], 16)

                def step(t, half, b, prep, edges, nodes, s=s, table=table, to=to):
                    if before_end(t, 2):
                        sp.wait_ge(s["scaled"], BLOCKS * (t + 1))
                        sp.wait_ge(s["vr"], t + 1)
                        sp.wait_ge(s["hot"], t + 1)
                        load_records(t + 2, b)
                    if edges:
                        if at_least(t, 1):
                            sp.wait_ge(s["z_full"], 4 * t)
                        if at_least(t, 2):
                            sp.wait_ge(s["h_ready"], t - 1)
                            sp.wait_ge(s["q_mul"], t - 1)
                        sp.dma_start(xt[b][0:HM, :], table[bass.ds(t * HM, HM), :]).then_inc(s["x_in"][b], 16)
                    if prep:
                        load_spill_sums(t + 1, 1 - b)
                    if at_least(t, 2):
                        sp.wait_ge(s["normed"], t - 1)
                        sp.dma_start(to[bass.ds((t - 2) * HM, HM), :], res[b][0:HM, :]).then_inc(s["stored"][b], 16)

                load_records(0, 0)
                load_records(1, 1)
                load_spill_sums(0, 0)
                sweep(sp, step)
                sp.wait_ge(s["normed"], tiles)
                sp.dma_start(to[(tiles - 1) * HM:tiles * HM, :], res[1][0:HM, :]).then_inc(s["stored"][1], 16)
            for b in range(2):
                sp.wait_ge(LS[1]["stored"][b], 16 * (tiles // 2))

        @block.gpsimd
        def _(g):
            g.memset(so.src_i[:, :], N).then_inc(padded, 1)
            g.memset(so.dst_i[:, :], 0).then_inc(padded, 1)
            g.memset(so.attr[:, :], 0.0).then_inc(padded, 1)
            g.iota(so.iota_i[:, :], [[1, NT]], base=0, channel_multiplier=0).then_inc(iotas, 1)
            g.iota(so.spill_row_i[:, :], [[0, 1]], base=SPILL0 - P, channel_multiplier=1).then_inc(iotas, 1)
            g.iota(node_iota_i[:, :], [[1, TILE_NODES]], base=0, channel_multiplier=0).then_inc(iotas, 1)
            g.iota(trash_i[:, :], [[0, 1]], base=TRASH, channel_multiplier=1).then_inc(iotas, 1)
            g.memset(ones_f[:, :], 1.0).then_inc(iotas, 1)
            g.memset(so.ones[:, :], 1.0).then_inc(iotas, 1)
            g.wait_ge(iotas, 6)
            g.affine_select(so.after[:, :], so.ones[:, :], [[1, P]], ALU.is_gt, 0.0, base=0, channel_multiplier=-1).then_inc(iotas, 1)
            g.affine_select(after[:, :], ones_f[:, :], [[1, P]], ALU.is_gt, 0.0, base=0, channel_multiplier=-1).then_inc(iotas, 1)
            g.affine_select(ident[:, :], ones_f[:, :], [[1, P]], ALU.is_equal, 0.0, base=0, channel_multiplier=-1).then_inc(iotas, 1)
            last_slot = g.to_reg(SLOTS - 1)
            def carry():
                g.sem_inc(dma_go, 1)

            g.wait_ge(emptied, 16 * FILLS)
            with g.Fori(0, STEPS) as i:
                for b in range(COUNT_BUFS):
                    c = COUNT_BUFS * i + b
                    g.wait_ge(ranked, c + 1)
                    g.wait_ge(packed, 4 * c + 4)
                    carry()
                    for j in range(COUNT_COLS):
                        g.indirect_dma_start(out=slots[:, :], out_offset=bass.IndirectOffsetOnAxis(ap=so.slot[:, b, j:j + 1], axis=0),
                                             in_=so.rec[:, b, j, :], in_offset=None, bounds_check=last_slot, oob_is_err=False
                                             ).then_inc(scattered[b], 16)
            for b in range(COUNT_BUFS):
                g.wait_ge(scattered[b], 16 * COUNT_COLS * STEPS)
            g.wait_ge(zeroed, 16 * 2 * ZEROS)
            g.nop().then_inc(sort_done, 1)
            g.wait_ge(flag_ready, 1)
            n_spill = g.value_load(spill_blocks[0:1, 0:1], min_val=0, max_val=COLS)

            for layer in range(2):
                s = LS[layer]
                table = x if layer == 0 else x_mid
                if layer == 1:
                    for b in range(2):
                        g.wait_ge(LS[0]["stored"][b], 16 * (tiles // 2))
                with g.If(n_spill > 0):
                    with g.Fori(0, n_spill) as k:
                        g.wait_ge(s["sp_rec"], 16 * k + 16)
                        carry()
                        g.indirect_dma_start(out=feat[1][:, 0, 0:D], out_offset=None, in_=table[:, :],
                                             in_offset=bass.IndirectOffsetOnAxis(ap=spill_rec[:, 0:1].bitcast(I32), axis=0)
                                             ).then_inc(s["sp_x"], 16)
                        g.wait_ge(s["sp_idx"], k + 1)
                        carry()
                        g.indirect_dma_start(out=spill_rows[:, :], out_offset=None, in_=spill_sums_of[layer][:, :],
                                             in_offset=bass.IndirectOffsetOnAxis(ap=spill_idx[:, :], axis=0)
                                             ).then_inc(s["sp_old"], 16)
                        g.wait_ge(s["sp_new"], 2 * k + 2)
                        carry()
                        g.indirect_dma_start(out=spill_sums_of[layer][:, :], out_offset=bass.IndirectOffsetOnAxis(ap=spill_idx[:, :], axis=0),
                                             in_=spill_rows[:, :], in_offset=None).then_inc(s["sp_put"], 16)
                    g.wait_ge(s["sp_put"], 16 * n_spill)
                g.nop().then_inc(s["sp_done"], 1)

                def gather(ks, half, b, *free, s=s, table=table):
                    for f in free:
                        g.wait_ge(*f)
                    g.wait_ge(s["rec_in"][b], 16 * half + 16)
                    carry()
                    for k in ks:
                        g.indirect_dma_start(out=feat[b][:, k, RAW:RAW + D], out_offset=None, in_=table[:, :],
                                             in_offset=bass.IndirectOffsetOnAxis(ap=recs[b][:, k, 0:1].bitcast(I32), axis=0)
                                             ).then_inc(s["gathered"][b], 16)

                def vector_products(n, nb, nh, s=s):
                    g.wait_ge(s["x_in"][nb], 16 * nh + 16)
                    g.wait_ge(s["y_out"], 4 * n + 4)
                    g.wait_ge(s["q_ready"], n)
                    g.tensor_tensor(q3[0:HM, :].rearrange("p (i u v) -> p i u v", i=3, u=V),
                                    xt[nb][0:HM, S:D].rearrange("p (u i) -> p i u", i=3).unsqueeze(3).broadcast_to([HM, 3, V, V]),
                                    yv[nb][0:HM, :, 0:V].unsqueeze(2).broadcast_to([HM, 3, V, V]), ALU.mult).then_inc(s["q_mul"], 1)
                    g.wait_ge(s["q_mul"], n + 1)
                    g.wait_ge(s["q_turned"], 2 * n)
                    g.tensor_tensor(q[0:HM, :], q3[0:HM, 0:VV], q3[0:HM, VV:2 * VV], ALU.add).then_inc(s["q_add"], 1)
                    g.wait_ge(s["q_add"], n + 1)
                    g.tensor_tensor(q[0:HM, :], q[0:HM, :], q3[0:HM, 2 * VV:3 * VV], ALU.add).then_inc(s["q_ready"], 1)

                def add_spilled(n, nb, nh, s=s):
                    g.wait_ge(s["spill_in"][nb], 16 * nh + 16)
                    z = sums[0:HM, :]
                    groups = z[:, P:4 * P].rearrange("p (i f) -> p i f", i=3)
                    more = spill_in[nb][0:HM, :]
                    lo = more[:, 0:HALF].rearrange("p (c f) -> p c f", c=2)
                    pairs = ((z[:, 0:P].rearrange("p (c f) -> p c f", c=2), lo[:, :, 0:S]),
                             (groups[:, :, S:P].rearrange("p i (c u) -> p i c u", c=2),
                              lo[:, :, S:D].rearrange("p c (u i) -> p i c u", i=3)),
                             (groups[:, :, 0:S], more[:, RS:FEAT].rearrange("p (i f) -> p i f", i=3)),
                             (z[:, 4 * P:FEAT], more[:, VR:VR + V]))
                    for k, (to, add) in enumerate(pairs):
                        g.wait_ge(s["z_out"], 4 * n + k + 1)
                        g.tensor_tensor(to, to, add, ALU.add).then_inc(s["z_full"], 1)

                first, second = range(0, SPLIT), range(SPLIT, BLOCKS)

                def step(t, half, b, prep, edges, nodes, s=s):
                    if nodes:
                        add_spilled(t - 1, 1 - b, half if b == 1 else half - 1)
                    if prep and at_least(t, 1):
                        gather(second, *following(half, b), (s["edges_done"], t))
                    if nodes:
                        vector_products(t - 1, 1 - b, half if b == 1 else half - 1)
                    if before_end(t, 2):
                        gather(first, half + 1, b, (s["edges_half"], t + 1))

                gather(range(BLOCKS), 0, 0)
                gather(range(BLOCKS), 0, 1)
                sweep(g, step)

        @block.vector
        def _(ve):
            ve.memset(so.empty[:, :, :], 0.0).then_inc(empty_made, 1)
            ve.wait_ge(empty_made, 1)
            ve.memset(so.empty[:, :, 1:2], -1.0).then_inc(empty_made, 1)
            for layer in range(2):
                for z in (wt[layer].bil[:, :], wt[layer].lin0[:, :], wt[layer].lin1[:, :]):
                    last = ve.memset(z, 0.0)
            last.then_inc(w_zeroed, 1)
            ve.memset(eps_col[:, :], EPS)
            ve.memset(so.onehot[:, :, :, :], 0.0)
            ve.memset(so.before[:, :, :], 0.0)
            ve.memset(so.spills[:, :, :], 0.0)
            ve.memset(so.ones_row[:, :], 1.0)
            ve.memset(so.zero[:, :], 0.0).then_inc(zero_made, 1)
            ve.memset(so.rec[:, :, :, :], 0.0).then_inc(consts, 1)
            ve.wait_ge(iotas, 4)
            ve.tensor_copy(so.iota[:, :], so.iota_i[:, :])
            ve.tensor_copy(trash[:, :], trash_i[:, :])
            ve.tensor_copy(node_iota[:, :], node_iota_i[:, :]).then_inc(consts, 1)
            ve.wait_ge(src_in, 16 * 2)
            n = 0

            def chain(ins):
                nonlocal n
                n += 1
                ins.then_inc(keyed, 1)
                ve.wait_ge(keyed, n)

            bk, lo, tmp = so.bucket[:, :], so.local[:, :], so.tmp[:, :]
            chain(ve.tensor_copy(so.src[:, :], so.src_i[:, :]))
            chain(ve.tensor_scalar(tmp, so.src[:, :], 0.5, 1.0 / TILE_NODES, ALU.add, ALU.mult))
            chain(ve.tensor_scalar(so.bucket_i[:, :], tmp, -0.5, None, ALU.add))
            chain(ve.tensor_copy(bk, so.bucket_i[:, :]))
            chain(ve.scalar_tensor_tensor(lo, bk, -float(TILE_NODES), so.src[:, :], ALU.mult, ALU.add))
            chain(ve.tensor_scalar(tmp, lo, 0.0, None, ALU.is_lt))
            chain(ve.tensor_tensor(bk, bk, tmp, ALU.subtract))
            chain(ve.tensor_scalar(tmp, lo, float(TILE_NODES), None, ALU.is_ge))
            chain(ve.tensor_tensor(bk, bk, tmp, ALU.add))
            chain(ve.scalar_tensor_tensor(lo, bk, -float(TILE_NODES), so.src[:, :], ALU.mult, ALU.add))
            chain(ve.tensor_copy(so.spill_row[:, :], so.spill_row_i[:, :]))
            chain(ve.tensor_scalar(tmp, bk, float(NT), float(1 << 20), ALU.is_ge, ALU.mult))
            chain(ve.scalar_tensor_tensor(so.base[:, :], bk, float(CAP), tmp, ALU.mult, ALU.add))
            ve.nop().then_inc(keys_ready, 1)
            LINKS = 4 * COUNT_BUFS + 6 * (COUNT_BUFS // 2)

            def bucket_rows(c, pb):
                ve.tensor_tensor(so.onehot[:, pb, 0:COUNT_COLS, :],
                                 so.bucket[:, bass.ds(c * COUNT_COLS, COUNT_COLS)].unsqueeze(2).broadcast_to([P, COUNT_COLS, NT]),
                                 so.iota[:, :].unsqueeze(1).broadcast_to([P, COUNT_COLS, NT]), ALU.is_equal).then_inc(hot, 1)

            def rank_groups(i, last):
                m = 0

                def link(ins):
                    nonlocal m
                    m += 1
                    ins.then_inc(ranking, 1)
                    ve.wait_ge(ranking, LINKS * i + m)

                for b in range(COUNT_BUFS):
                    c = COUNT_BUFS * i + b
                    pb = b % 2
                    hots = so.onehot[:, pb, 0:COUNT_COLS, :]
                    cnt = (sum_lo, sum_hi)[pb][:, 0:(COUNT_COLS + 1) * NT].rearrange("p (j b) -> p j b", b=NT)
                    if not (last and b == COUNT_BUFS - 1):
                        bucket_rows(c + 1, 1 - pb)
                    ve.wait_ge(counted, c + 1)
                    pick = so.pick[:, pb, :, :]
                    link(ve.tensor_tensor(so.before[:, 1 - pb, :], so.before[:, pb, :], cnt[:, COUNT_COLS, :], ALU.add))
                    link(ve.tensor_tensor(pick, cnt[:, 0:COUNT_COLS, :],
                                          so.before[:, pb, :].unsqueeze(1).broadcast_to([P, COUNT_COLS, NT]), ALU.add))
                    link(ve.tensor_tensor(pick, pick, hots, ALU.mult))
                    link(ve.tensor_reduce(so.rank[:, b, :], pick, AX_X, ALU.add))
                    if pb == 0:
                        continue
                    pair, cols = slice(b - 1, b + 1), bass.ds((c - 1) * COUNT_COLS, 2 * COUNT_COLS)
                    rank, so_far, slot = (z[:, pair, :].rearrange("p a j -> p (a j)") for z in (so.rank, so.spills, so.slot))
                    pl = [so.place[:, b // 2, k, :] for k in range(4)]
                    link(ve.tensor_scalar(pl[0], rank, float(CAP), None, ALU.is_ge))
                    link(ve.tensor_tensor_scan(so_far, so.ones_row[:, :], pl[0], so.spills[:, (b - 2) % COUNT_BUFS, COUNT_COLS - 1:COUNT_COLS], ALU.mult, ALU.add))
                    link(ve.tensor_tensor(pl[1], so.base[:, cols], rank, ALU.add))
                    link(ve.tensor_scalar(pl[2], so_far, float(P), so.spill_row[:, :], ALU.mult, ALU.add))
                    link(ve.tensor_tensor(pl[2], pl[2], pl[1], ALU.subtract))
                    link(ve.tensor_tensor(pl[3], pl[0], pl[2], ALU.mult))
                    for k in (b - 1, b):
                        ve.wait_ge(scattered[k], 16 * COUNT_COLS * i)
                    ve.tensor_tensor(slot, pl[1], pl[3], ALU.add).then_inc(ranked, 2)
                assert m == LINKS

            bucket_rows(0, 0)
            with ve.Fori(0, STEPS - 1) as i:
                rank_groups(i, False)
            rank_groups(STEPS - 1, True)
            ve.wait_ge(spills_turned, 1)
            ve.tensor_reduce(most[0:1, :], small_ps[0:1, 0:P], AX_X, ALU.max).then_inc(keyed, 1)
            ve.wait_ge(keyed, n + 1)
            ve.tensor_copy(spill_blocks[0:1, :], most[0:1, :]).then_inc(flag_ready, 1)

            def scale_weights():
                ve.wait_ge(w_in, 16 * 14 * 2)
                for layer in range(2):
                    k, t = layer_scales(layer), wt[layer]
                    mix = t.bil[:, SS:SS + MIX]
                    for part, c in ((t.bil[S:P, 0:SS], "u_ss"), (mix[0:S, :], "u_sv"), (mix[S:P, :], "u_vs"),
                                    (t.vv[:, :, :], "u_vv"), (t.msg0[0:S, :], "l_s"), (t.msg0[S:P, :], "m_ss"),
                                    (t.msg1[0:S, :], "m_sv"), (t.msg1[S:S + V, :], "l_v"), (t.msg1[S + V:P, :], "m_vs"),
                                    (t.msg_vr[:, :], "m_vv"), (t.lin0[0:S, :], "l_s"), (t.lin1[:, :], "l_v")):
                        last = ve.tensor_scalar(part, part, float(k[c]), None, ALU.mult)
                last.then_inc(w_ready, 1)

            ve.wait_ge(flag_ready, 1)
            n_spill = ve.value_load(spill_blocks[0:1, 0:1], min_val=0, max_val=COLS)

            for layer in range(2):
                s = LS[layer]
                SPILL_LINKS = 16
                with ve.If(n_spill > 0):
                    if layer == 1:
                        ve.wait_ge(LS[0]["edges_done"], tiles)
                    else:
                        ve.wait_ge(sort_done, 1)
                    with ve.Fori(0, n_spill) as k:
                        m = 0

                        def link(ins, s=s, k=k):
                            nonlocal m
                            m += 1
                            ins.then_inc(s["sp_link"], 1)
                            ve.wait_ge(s["sp_link"], SPILL_LINKS * k + m)

                        f = feat[1][:, 0, :]
                        key, c8 = spill_rec[:, 6:7], [spill_key[:, j:j + 1] for j in range(8)]
                        ve.wait_ge(s["sp_rec"], 16 * k + 16)
                        link(ve.tensor_scalar(c8[0], spill_rec[:, 1:2], 0.0, None, ALU.is_ge))
                        link(ve.tensor_scalar(c8[1], c8[0], 1.0, None, ALU.subtract))
                        link(ve.scalar_tensor_tensor(c8[2], key, c8[0], c8[1], ALU.mult, ALU.add))
                        ve.tensor_scalar(spill_same[:, 0, :], ident[:, :], c8[2], None, ALU.mult).then_inc(s["sp_diag"], 1)
                        ve.wait_ge(s["sp_keys"], k + 1)
                        link(ve.tensor_scalar(spill_same[:, 1, :], small_ps[:, 0:P], c8[2], None, ALU.is_equal))
                        link(ve.tensor_tensor(spill_same[:, 0, :], spill_same[:, 1, :], after[:, :], ALU.mult))
                        link(ve.tensor_reduce(c8[3], spill_same[:, 0, :], AX_X, ALU.add))
                        link(ve.tensor_scalar(c8[4], c8[3], 0.0, None, ALU.is_equal))
                        link(ve.tensor_tensor(c8[4], c8[4], c8[0], ALU.mult))
                        link(ve.tensor_tensor(c8[5], key, trash[:, :], ALU.subtract))
                        link(ve.tensor_tensor(c8[6], c8[5], c8[4], ALU.mult))
                        ve.tensor_tensor(spill_idx[:, :], c8[6], trash[:, :], ALU.add).then_inc(s["sp_idx"], 1)
                        ve.wait_ge(s["sp_x"], 16 * k + 16)
                        vec = f[:, S:D].rearrange("p (u i) -> p u i", i=3)
                        link(ve.tensor_scalar(f[:, DIST:DIST + D], f[:, 0:D], spill_rec[:, 5:6], None, ALU.mult))
                        link(ve.tensor_scalar(f[:, VR:VR + V], vec[:, :, 0], spill_rec[:, 2:3], None, ALU.mult))
                        link(ve.scalar_tensor_tensor(f[:, VR:VR + V], vec[:, :, 1], spill_rec[:, 3:4], f[:, VR:VR + V], ALU.mult, ALU.add))
                        link(ve.scalar_tensor_tensor(f[:, VR:VR + V], vec[:, :, 2], spill_rec[:, 4:5], f[:, VR:VR + V], ALU.mult, ALU.add))
                        for i in range(3):
                            rs = ve.tensor_scalar(f[:, RS + S * i:RS + S * i + S], f[:, 0:S], spill_rec[:, 2 + i:3 + i], None, ALU.mult)
                            if i < 2:
                                link(rs)
                        rs.then_inc(s["sp_feat"], 1)
                        assert m == SPILL_LINKS
                        ve.wait_ge(s["sp_sum"], k + 1)
                        ve.wait_ge(s["sp_old"], 16 * k + 16)
                        ve.tensor_tensor(spill_rows[:, 0:HALF], spill_rows[:, 0:HALF], sum_lo[:, 0:HALF], ALU.add).then_inc(s["sp_new"], 1)
                        ve.tensor_tensor(spill_rows[:, HALF:FEAT], spill_rows[:, HALF:FEAT], sum_hi[:, 0:FEAT - HALF], ALU.add).then_inc(s["sp_new"], 1)
                if layer == 0:
                    scale_weights()
                ve.wait_ge(s["sp_done"], 1)

                def one_hot(t, half, b, s=s):
                    ve.wait_ge(s["rec_in"][b], 16 * half + 16)
                    if at_least(t, 2):
                        ve.wait_ge(s["edges_done"], t - 1)
                    ve.tensor_tensor(onehot[b][:, :, :], recs[b][:, :, 1:2].broadcast_to([P, BLOCKS, HM]),
                                     node_iota[:, :].unsqueeze(1).broadcast_to([P, BLOCKS, HM]), ALU.is_equal).then_inc(s["hot"], 1)

                def sum_vr(t, half, b, *free, s=s):
                    for f in free:
                        ve.wait_ge(*f)
                    ve.wait_ge(s["gathered"][b], 16 * BLOCKS * half + 16 * BLOCKS)
                    vr = work[:, 0:BLOCKS * 3 * V].rearrange("p (k u i) -> p k u i", u=V, i=3)
                    ve.tensor_tensor(vr, feat[b][:, :, S:D].rearrange("p k (u i) -> p k u i", i=3),
                                     recs[b][:, :, 2:5].unsqueeze(2).broadcast_to([P, BLOCKS, V, 3]), ALU.mult).then_inc(s["vr_mul"], 1)
                    ve.wait_ge(s["vr_mul"], t + 1)
                    ve.tensor_reduce(feat[b][:, :, VR:VR + V], vr, AX_X, ALU.add).then_inc(s["vr"], 1)

                def step(t, half, b, prep, edges, nodes, s=s):
                    if prep:
                        one_hot(t + 1, *following(half, b))
                    if not nodes:
                        sum_vr(t + 1, *following(half, b), (s["vr"], t + 1))
                        return
                    n, nb, nh = t - 1, 1 - b, (half if b == 1 else half - 1)
                    X = xt[nb][0:HM, :]
                    ve.wait_ge(s["x_in"][nb], 16 * nh + 16)
                    if at_least(n, 1) and at_least(t, 2):
                        ve.wait_ge(s["upd"], RS_ALL * n)
                    else:
                        ve.wait_ge(s["vr"], 2)
                    ve.wait_ge(s["h_part"], 3 * n)
                    ve.wait_ge(s["y_out"], 4 * n + 4)

                    def third(r):
                        return work[0:HM, ROUND * (r % 3):ROUND * (r % 3) + ROUND].rearrange("p (w u) -> p w u", u=S)

                    for r in range(R0 + 1):
                        if r < R0:
                            ve.wait_ge(s["prods"], RS_ALL * n + r + 1)
                            if r >= 3:
                                ve.wait_ge(s["upd"], RS_ALL * n + r - 2)
                            ve.tensor_tensor(third(r), prods_ps[r % 2][0:HM, :].rearrange("p (w u) -> p w u", u=S),
                                             X[:, 0:S].unsqueeze(1).broadcast_to([HM, ROUND // S, S]), ALU.mult).then_inc(s["prods_used"], 1)
                        if r > 0:
                            ve.wait_ge(s["prods_used"], USES * n + used(r - 1))
                            ve.tensor_reduce(upd[0:HM, ROUND // S * (r - 1):ROUND // S * r], third(r - 1), AX_X, ALU.add).then_inc(s["upd"], 1)
                    if at_least(t, 2):
                        normalise(t - 2, half - 1, b, s)
                    if prep:
                        sum_vr(t + 1, *following(half, b), (s["upd"], RS_ALL * n + R0))
                    wk = work[0:HM, :].rearrange("p (i w k) -> p i w k", i=3, k=KV)
                    upd1 = upd[0:HM, S:D].rearrange("p (w i) -> p i w", i=3)
                    for r in range(R0, R0 + R1):
                        ve.wait_ge(s["prods"], RS_ALL * n + r + 1)
                        ve.wait_ge(s["upd"], RS_ALL * n + r)
                        for i in (2, 0, 1):
                            if i == 0 and r == R0 and prep:
                                ve.wait_ge(s["vr"], t + 2)
                            ve.tensor_tensor(wk[:, i, :, :], prods_ps[r % 2][0:HM, :].rearrange("p (w k) -> p w k", k=KV),
                                             yv[nb][0:HM, i, :].unsqueeze(1).broadcast_to([HM, ROUND // KV, KV]), ALU.mult).then_inc(s["prods_used"], 1)
                        ve.wait_ge(s["prods_used"], USES * n + used(r))
                        w0 = ROUND // KV * (r - R0)
                        ve.tensor_reduce(upd1[:, :, w0:w0 + ROUND // KV], wk, AX_X, ALU.add).then_inc(s["upd"], 1)
                    ve.wait_ge(s["lin_out"], 2 * n + 2)
                    ve.wait_ge(s["normed"], n)
                    ve.scalar_tensor_tensor(h[0:HM, :], X, 2.0, lin[0:HM, :], ALU.mult, ALU.add).then_inc(s["h_part"], 1)
                    ve.wait_ge(s["upd"], RS_ALL * n + RS_ALL)
                    ve.wait_ge(s["h_part"], 3 * n + 1)
                    ve.tensor_tensor(h[0:HM, :], h[0:HM, :], upd[0:HM, :], ALU.add).then_inc(s["h_part"], 1)
                    ve.wait_ge(s["h_part"], 3 * n + 2)
                    ve.tensor_reduce(stats[0:HM, 0:1], h[0:HM, :], AX_X, ALU.add).then_inc(s["h_part"], 1)
                    ve.wait_ge(s["h_part"], 3 * n + 3)
                    ve.tensor_scalar(stats[0:HM, 1:2], stats[0:HM, 0:1], -1.0 / D, None, ALU.mult).then_inc(s["h_ready"], 1)

                def normalise(n, half, b, s):
                    ve.wait_ge(s["deviation"], n + 1)
                    ve.wait_ge(s["stored"][b], 16 * half)
                    ve.reciprocal(stats[0:HM, 4:5], stats[0:HM, 3:4]).then_inc(s["inverse"], 1)
                    ve.wait_ge(s["inverse"], n + 1)
                    ve.tensor_scalar(res[b][0:HM, :], h[0:HM, :], stats[0:HM, 1:2], stats[0:HM, 4:5], ALU.add, ALU.mult
                                     ).then_inc(s["normed"], 1)

                one_hot(0, 0, 0)
                sum_vr(0, 0, 0)
                sweep(ve, step)
                normalise(tiles - 1, tiles // 2 - 1, 1, s)

        @block.tensor
        def _(te):
            te.wait_ge(iotas, 9)
            te.wait_ge(consts, 1)
            with te.Fori(0, STEPS) as i:
                for b in range(COUNT_BUFS):
                    te.wait_ge(hot, COUNT_BUFS * i + b + 1)
                    cnt = (sum_lo, sum_hi)[b % 2][:, 0:(COUNT_COLS + 1) * NT]
                    hots = so.onehot[:, b % 2, :, :].rearrange("p j b -> p (j b)")
                    te.matmul(cnt, so.after[:, :], hots, start=True, stop=False)
                    for c in range(1, COUNT_COLS + 1):
                        mm = te.matmul(cnt[:, c * NT:], so.ones[:, :], hots[:, 0:(COUNT_COLS + 1 - c) * NT],
                                       start=False, stop=(c == COUNT_COLS))
                    mm.then_inc(counted, 1)
            te.wait_ge(ranked, COUNT_BUFS * STEPS)
            te.transpose(small_ps[0:1, 0:P], so.spills[:, COUNT_BUFS - 1, COUNT_COLS - 1:COUNT_COLS], ident[:, :]).then_inc(spills_turned, 1)
            te.wait_ge(flag_ready, 1)
            n_spill = te.value_load(spill_blocks[0:1, 0:1], min_val=0, max_val=COLS)
            for layer in range(2):
                s, w = LS[layer], wt[layer]
                with te.If(n_spill > 0):
                    with te.Fori(0, n_spill) as k:
                        te.wait_ge(s["sp_diag"], k + 1)
                        te.matmul(small_ps[:, 0:P], ones_f[:, :], spill_same[:, 0, :], start=True, stop=True).then_inc(s["sp_keys"], 1)
                        te.wait_ge(s["sp_feat"], k + 1)
                        te.matmul(sum_lo[:, 0:HALF], spill_same[:, 1, :], feat[1][:, 0, 0:HALF], start=True, stop=True)
                        te.matmul(sum_hi[:, 0:FEAT - HALF], spill_same[:, 1, :], feat[1][:, 0, HALF:FEAT],
                                  start=True, stop=True).then_inc(s["sp_sum"], 1)
                te.wait_ge(w_ready, 1)
                te.wait_ge(s["sp_done"], 1)

                def sum_edges(t, half, b, ks, s=s):
                    for k in ks:
                        if k == 0:
                            te.wait_ge(s["hot"], t + 1)
                            te.wait_ge(s["vr"], t + 1)
                        te.wait_ge(s["scaled"], BLOCKS * t + k + 1)
                        lhs = onehot[b][:, k, :]
                        te.matmul(sum_lo[0:HM, 0:HALF], lhs, feat[b][:, k, 0:HALF], start=(k == 0), stop=(k == BLOCKS - 1))
                        mm = te.matmul(sum_hi[0:HM, 0:FEAT - HALF], lhs, feat[b][:, k, HALF:FEAT], start=(k == 0), stop=(k == BLOCKS - 1))
                        if k == SPLIT - 1:
                            mm.then_inc(s["edges_half"], 1)
                        if k == BLOCKS - 1:
                            mm.then_inc(s["edges_done"], 1)

                def step(t, half, b, prep, edges, nodes, s=s, w=w):
                    def some_edges(k0, k1):
                        if edges:
                            sum_edges(t, half, b, range(k0, k1))

                    if not nodes:
                        some_edges(0, BLOCKS)
                        return
                    n = t - 1
                    nb = 1 - b
                    idn = ident[0:HM, 0:HM]

                    def turn_q(part):
                        for c in range(QC // 2):
                            mm = te.transpose(turn_ps[:, HM * c:HM * c + HM], q[0:HM, P * (c + part * QC // 2):P * (c + part * QC // 2 + 1)], idn)
                        mm.then_inc(s["q_turned"], 1)

                    def bilinear(r):
                        if r >= 2:
                            te.wait_ge(s["prods_used"], USES * n + used(r - 2))
                        elif at_least(n, 1) and at_least(t, 2):
                            te.wait_ge(s["prods_used"], USES * n - USES + used(r + RS_ALL - 2))
                        for hh in range(2):
                            c = ROUND * r + 512 * hh
                            rows = slice(S, P) if c < SS else slice(0, P)
                            mm = te.matmul(prods_ps[r % 2][0:HM, 512 * hh:512 * hh + 512], ys_t[rows, :], w.bil[rows, c:c + 512],
                                           start=True, stop=True)
                        mm.then_inc(s["prods"], 1)

                    te.wait_ge(s["z_full"], 4 * n + 4)
                    te.wait_ge(s["q_turned_out"], 2 * n)
                    for c in range(4):
                        te.transpose(turn_ps[:, HM * c:HM * c + HM], sums[0:HM, P * c:P * c + P], idn)
                    te.wait_ge(s["lin_out"], 2 * n)
                    te.transpose(small_ps[0:V, VRT], sums[0:HM, 4 * P:FEAT], idn).then_inc(s["turned"], 1)
                    some_edges(0, 2)
                    te.wait_ge(s["turned_out"], 2 * n + 2)
                    te.matmul(small_ps[0:HM, D:D + S], sums_t[:, 0:HM], w.msg0[:, :], start=True, stop=False)
                    te.matmul(small_ps[0:HM, D:D + S], vr_t[:, :], w.msg_vr[:, :], start=False, stop=True)
                    for i in range(3):
                        mm = te.matmul(small_ps[0:HM, D + S + V * i:D + S + V * i + V], sums_t[:, HM * (i + 1):HM * (i + 2)], w.msg1[:, :],
                                       start=True, stop=True)
                    mm.then_inc(s["agg"], 1)
                    some_edges(2, 3)
                    te.wait_ge(s["y_out"], 4 * n + 4)
                    te.transpose(turn_ps[:, 0:HM], ys[nb][0:HM, :], idn)
                    te.transpose(turn_ps[0:3 * V, HM:2 * HM], yx[nb][0:HM, :], idn).then_inc(s["y_turned"], 1)
                    some_edges(3, 4)
                    te.wait_ge(s["y_turned_out"], 2 * n + 2)
                    bilinear(0)
                    bilinear(1)
                    some_edges(4, 6)
                    bilinear(2)
                    some_edges(6, 7)
                    bilinear(3)
                    some_edges(7, 10)
                    te.wait_ge(s["q_ready"], n + 1)
                    turn_q(0)
                    bilinear(4)
                    some_edges(10, 12)
                    te.wait_ge(s["q_turned_out"], 2 * n + 1)
                    turn_q(1)
                    some_edges(12, BLOCKS)
                    bilinear(5)
                    te.wait_ge(s["q_turned_out"], 2 * n + 2)
                    te.matmul(small_ps[0:HM, S:D], v_t[:, :], w.lin1[:, :], start=True, stop=True)
                    te.matmul(small_ps[0:HM, 0:S], ys_t[:, :], w.lin0[:, :], start=True, stop=False)
                    for c in range(QC):
                        mm = te.matmul(small_ps[0:HM, 0:S], q_t[:, c, :], w.vv[:, c, :], start=False, stop=(c == QC - 1))
                    mm.then_inc(s["lin"], 1)

                sweep(te, step)

        @block.scalar
        def _(ac):
            ac.wait_ge(keys_ready, 1)
            ac.wait_ge(edges_in, 16 * 4)
            with ac.Fori(0, STEPS) as i:
                for b in range(COUNT_BUFS):
                    o = (COUNT_BUFS * i + b) * COUNT_COLS
                    cols = bass.ds(o, COUNT_COLS)
                    ac.wait_ge(scattered[b], 16 * COUNT_COLS * i)
                    ac.copy(so.rec[:, b, :, 0:1].bitcast(I32), so.dst_i[:, cols].unsqueeze(2)).then_inc(packed, 1)
                    ac.copy(so.rec[:, b, :, 1:2], so.local[:, cols].unsqueeze(2)).then_inc(packed, 1)
                    ac.copy(so.rec[:, b, :, 2:6], so.attr[:, bass.ds(o * 4, COUNT_COLS * 4)].rearrange("p (j f) -> p j f", f=4)
                            ).then_inc(packed, 1)
                    ac.copy(so.rec[:, b, :, 6:7], so.src[:, cols].unsqueeze(2)).then_inc(packed, 1)
            for layer in range(2):
                s = LS[layer]

                def deviation(n, s=s):
                    ac.wait_ge(s["h_ready"], n + 1)
                    ac.activation(sq[0:HM, :], h[0:HM, :], ACT.Square, bias=stats[0:HM, 1:2], accum_out=stats[0:HM, 2:3]).then_inc(s["squares"], 1)
                    ac.wait_ge(s["squares"], n + 1)
                    ac.activation(stats[0:HM, 3:4], stats[0:HM, 2:3], ACT.Sqrt, bias=eps_col[0:HM, :], scale=1.0 / D).then_inc(s["deviation"], 1)

                def scale_edges(t, half, b, ks, s=s):
                    for k in ks:
                        if k == 0:
                            ac.wait_ge(s["gathered"][b], 16 * BLOCKS * half + 16 * BLOCKS)
                        f = feat[b][:, k, :]
                        ac.activation(f[:, DIST:DIST + D], f[:, RAW:RAW + D], ACT.Copy, scale=recs[b][:, k, 5:6])
                        for i in range(3):
                            last = ac.activation(f[:, RS + S * i:RS + S * i + S], f[:, RAW:RAW + S], ACT.Copy, scale=recs[b][:, k, 2 + i:3 + i])
                        last.then_inc(s["scaled"], 1)

                FIRST = 6

                def linear_part(n, s=s):
                    ac.wait_ge(s["lin"], n + 1)
                    ac.wait_ge(s["h_part"], 3 * n)
                    ac.copy(lin[0:HM, 0:S], small_ps[0:HM, 0:S]).then_inc(s["lin_out"], 1)
                    ac.copy(lin[0:HM, S:D].rearrange("p (u i) -> p u i", i=3),
                            small_ps[0:HM, S:D].rearrange("p (i u) -> p u i", i=3)).then_inc(s["lin_out"], 1)

                def step(t, half, b, prep, edges, nodes, s=s):
                    def scale_next(k0, k1):
                        if prep:
                            scale_edges(t + 1, *following(half, b), range(k0, k1))

                    if not nodes:
                        scale_next(0, FIRST)
                        return
                    n, nb, nh = t - 1, 1 - b, (half if b == 1 else half - 1)
                    ac.wait_ge(s["x_in"][nb], 16 * nh + 16)
                    if at_least(t, 3):
                        ac.wait_ge(s["y_turned"], n - 1)
                        ac.wait_ge(s["prods_used"], USES * (n - 1))
                        ac.wait_ge(s["q_mul"], n - 1)
                    xv = xt[nb][0:HM, S:D].rearrange("p (u i) -> p i u", i=3)
                    ac.copy(ys[nb][0:HM, 0:S], xt[nb][0:HM, 0:S]).then_inc(s["y_out"], 1)
                    ac.copy(yx[nb][0:HM, :].rearrange("p (i u) -> p i u", i=3), xv)
                    ac.copy(yv[nb][0:HM, :, V:KV], xv).then_inc(s["y_out"], 1)
                    ac.wait_ge(s["edges_done"], n + 1)
                    lo = sum_lo[0:HM, 0:HALF].rearrange("p (c f) -> p c f", c=2)
                    groups = sums[0:HM, P:4 * P].rearrange("p (i f) -> p i f", i=3)
                    ac.copy(sums[0:HM, 0:P].rearrange("p (c f) -> p c f", c=2), lo[:, :, 0:S]).then_inc(s["z_out"], 1)
                    ac.copy(groups[:, :, S:P].rearrange("p i (c u) -> p i c u", c=2),
                            lo[:, :, S:D].rearrange("p c (u i) -> p i c u", i=3)).then_inc(s["z_out"], 1)
                    ac.copy(groups[:, :, 0:S], sum_hi[0:HM, V:V + 3 * S].rearrange("p (i f) -> p i f", i=3)).then_inc(s["z_out"], 1)
                    ac.copy(sums[0:HM, 4 * P:FEAT], sum_hi[0:HM, 0:V]).then_inc(s["z_out"], 1)
                    if at_least(t, 2):
                        linear_part(t - 2)
                    ac.wait_ge(s["turned"], n + 1)
                    ac.copy(sums_t[:, :], turn_ps[:, 0:4 * HM]).then_inc(s["turned_out"], 1)
                    ac.copy(vr_t[:, :], small_ps[0:V, VRT]).then_inc(s["turned_out"], 1)
                    ac.wait_ge(s["agg"], n + 1)
                    ac.copy(ys[nb][0:HM, S:2 * S], small_ps[0:HM, D:D + S]).then_inc(s["y_out"], 1)
                    ac.copy(yv[nb][0:HM, :, 0:V], small_ps[0:HM, D + S:2 * D].rearrange("p (i u) -> p i u", i=3)).then_inc(s["y_out"], 1)
                    ac.wait_ge(s["y_turned"], n + 1)
                    ac.copy(ys_t[:, :], turn_ps[:, 0:HM]).then_inc(s["y_turned_out"], 1)
                    ac.copy(v_t[:, :], turn_ps[0:3 * V, HM:2 * HM]).then_inc(s["y_turned_out"], 1)
                    if not at_least(t, 2):
                        scale_edges(t, half, b, range(FIRST, BLOCKS))
                    if at_least(t, 2):
                        deviation(t - 2)
                    for part, (k0, k1) in enumerate(((0, 11), (11, 13))):
                        scale_next(k0, k1)
                        ac.wait_ge(s["q_turned"], 2 * n + part + 1)
                        ac.copy(q_t[:, QC // 2 * part:QC // 2 * (part + 1), :], turn_ps[:, 0:QC // 2 * HM].rearrange("p (c n) -> p c n", n=HM)
                                ).then_inc(s["q_turned_out"], 1)
                    scale_next(13, BLOCKS)

                scale_edges(0, 0, 0, range(0, BLOCKS))
                sweep(ac, step)
                linear_part(tiles - 1)
                deviation(tiles - 1)


_WEIGHTS = {
    "m_ss": ("L0_gnn_wm000", "L1_gnn_Wm_ss"), "m_vv": ("L0_gnn_wm110", "L1_gnn_Wm_vv"),
    "m_sv": ("L0_gnn_wm011", "L1_gnn_Wm_sv"), "m_vs": ("L0_gnn_wm101", "L1_gnn_Wm_vs"),
    "lm_s": ("L0_gnn_lm0", "L1_gnn_Lm_s"), "lm_v": ("L0_gnn_lm1", "L1_gnn_Lm_v"),
    "lu_s": ("L0_gnn_lu0", "L1_gnn_Lu_s"), "lu_v": ("L0_gnn_lu1", "L1_gnn_Lu_v"),
    "u_ss": ("L0_gnn_wu000", "L1_gnn_Wu_ss"), "u_sv": ("L0_gnn_wu011", "L1_gnn_Wu_sv"),
    "u_vs": ("L0_gnn_wu101", "L1_gnn_Wu_vs"), "u_vv": ("L0_gnn_wu110", "L1_gnn_Wu_vv"),
}


def laid_out(name, a):
    if name in ("u_ss", "u_vs"):
        a = a.transpose(1, 2, 0)
        return np.ascontiguousarray(a.reshape(S, SS) if name == "u_ss" else a)
    if name == "u_sv":
        return np.ascontiguousarray(a.transpose(0, 2, 1))
    if name == "u_vv":
        return np.ascontiguousarray(a.reshape(V * V, S))
    return np.ascontiguousarray(a.reshape(-1, a.shape[-1]))


def kernel(**inputs):
    import concourse.bacc as bacc
    from concourse.bass_utils import run_bass_kernel_spmd

    nc = bacc.Bacc("TRN2", target_bir_lowering=False, num_devices=1)
    arrays = {}

    def given(name, a):
        arrays[name] = a
        return nc.dram_tensor(name, a.shape, mybir.dt.from_np(a.dtype), kind="ExternalInput").ap()

    x = given("x", np.ascontiguousarray(inputs["x"]))
    src = given("src", np.ascontiguousarray(inputs["src"]))
    dst = given("dst", np.ascontiguousarray(inputs["dst"]))
    attr = given("edge_attr", np.ascontiguousarray(inputs["edge_attr_4"]).reshape(-1))
    weights = [{k: given(f"{k}_{layer}", laid_out(k, np.asarray(inputs[names[layer]])))
                for k, names in _WEIGHTS.items()} for layer in range(2)]
    out = nc.dram_tensor("out", inputs["x"].shape, F32, kind="ExternalOutput").ap()
    build(nc, x, src, dst, attr, weights, out)
    r = run_bass_kernel_spmd(nc, [arrays], core_ids=[0])
    return r.results[0]["out"]
```
